# Optimizing a Trainium2 kernel written in Bass

```python
import numpy as np
import jax
import jax.numpy as jnp

def _softmax(x, axis=-1):
    return jax.nn.softmax(x, axis=axis)

def _gelu(x):
    return jax.nn.gelu(x, approximate=True)

def _silu(x):
    return jax.nn.silu(x)

def _sigmoid(x):
    return jax.nn.sigmoid(x)

def _layernorm(x, axis=-1, eps=1e-05):
    m = jnp.mean(x, axis=axis, keepdims=True)
    v = jnp.var(x, axis=axis, keepdims=True)
    return (x - m) / jnp.sqrt(v + eps)

def _scatter_add(tgt, idx, src, axis=0):
    return tgt.at[idx].add(src)

def _segment_sum(src, seg, n):
    return jax.ops.segment_sum(src, seg, n)
kernel_name = 'mk_gnn_resnorm_d2_gnn_r64_f16925'

def setup_inputs(seed: int=0):
    np.random.seed(seed)
    _w = jnp.asarray

    def _rec_inputs():
        import jax
        import jax.numpy as jnp
        _gk = jax.random.key(seed)
        x = -0.0003713 + 1 * jax.random.normal(jax.random.fold_in(_gk, 1), (100000, 128), jnp.float32)
        src = jax.random.randint(jax.random.fold_in(_gk, 2), (25000,), 0, 100000, jnp.int32)
        dst = jnp.minimum((100000 * jax.random.uniform(jax.random.fold_in(_gk, 3), (25000,)) ** 2.0).astype(jnp.int32), 99999)
        _o = jnp.argsort(dst, stable=True)
        src = src[_o]
        dst = dst[_o]
        return (x, src, dst)
    x, src, dst = _rec_inputs()

    def _L0_gnn_setup():
        import jax, jax.numpy as jnp
        import numpy as np
        N, E, C = (100000, 25000, 128)
        EPS = 1e-05

        def _bn(x, g, b):
            mu = jnp.mean(x, axis=0)
            var = jnp.mean((x - mu) ** 2, axis=0)
            return g * (x - mu) * jax.lax.rsqrt(var + EPS) + b
        key = jax.random.key(seed)
        ks = jax.random.split(key, 8)
        s = 1.0 / np.sqrt(C)
        return {'h': jax.random.normal(ks[0], (N, C), jnp.float32), 'src': jax.random.randint(ks[1], (E,), 0, N, jnp.int32), 'dst': jax.random.randint(ks[2], (E,), 0, N, jnp.int32), 'theta_w': jax.random.normal(ks[3], (C, C), jnp.float32) * s, 'phi_w': jax.random.normal(ks[4], (C, C), jnp.float32) * s, 'fc1_w': jax.random.normal(ks[5], (C, C), jnp.float32) * s, 'bn0_g': jnp.ones((C,), jnp.float32), 'bn0_b': jnp.zeros((C,), jnp.float32), 'bn1_g': jnp.ones((C,), jnp.float32), 'bn1_b': jnp.zeros((C,), jnp.float32)}
    _L0_gnn_all = _L0_gnn_setup()
    _L0_gnn_in = {k: v for k, v in _L0_gnn_all.items() if k in ('theta_w', 'phi_w', 'fc1_w', 'bn0_g', 'bn0_b', 'bn1_g', 'bn1_b')}
    del _L0_gnn_all

    def _L1_gnn_setup():
        import jax, jax.numpy as jnp
        import numpy as np
        N_NODES = 100000
        N_EDGES = 25000
        D_IN = 128
        D_HID = 128
        D_OUT = 128

        def _scatter_mean(feat, src, dst, n_nodes):
            summed = jax.ops.segment_sum(feat[src], dst, num_segments=n_nodes)
            deg = jax.ops.segment_sum(jnp.ones_like(dst, dtype=feat.dtype), dst, num_segments=n_nodes)
            return summed / jnp.maximum(deg, 1.0)[:, None]

        def _sage_conv(x, src, dst, Wl, bl, Wr):
            agg = _scatter_mean(x, src, dst, x.shape[0])
            return agg @ Wl.T + bl + x @ Wr.T
        key = jax.random.key(seed)
        ks = jax.random.split(key, 8)
        x = jax.random.normal(ks[0], (N_NODES, D_IN), dtype=jnp.float32)
        edge_index = jax.random.randint(ks[1], (2, N_EDGES), 0, N_NODES, dtype=jnp.int64)
        s = 1.0 / np.sqrt(D_IN)
        W1l = jax.random.uniform(ks[2], (D_HID, D_IN), jnp.float32, -s, s)
        b1l = jax.random.uniform(ks[3], (D_HID,), jnp.float32, -s, s)
        W1r = jax.random.uniform(ks[4], (D_HID, D_IN), jnp.float32, -s, s)
        s2 = 1.0 / np.sqrt(D_HID)
        W2l = jax.random.uniform(ks[5], (D_OUT, D_HID), jnp.float32, -s2, s2)
        b2l = jax.random.uniform(ks[6], (D_OUT,), jnp.float32, -s2, s2)
        W2r = jax.random.uniform(ks[7], (D_OUT, D_HID), jnp.float32, -s2, s2)
        return {'x': x, 'edge_index': edge_index, 'W1l': W1l, 'b1l': b1l, 'W1r': W1r, 'W2l': W2l, 'b2l': b2l, 'W2r': W2r}
    _L1_gnn_all = _L1_gnn_setup()
    _L1_gnn_in = {k: v for k, v in _L1_gnn_all.items() if k in ('W1l', 'b1l', 'W1r', 'W2l', 'b2l', 'W2r')}
    del _L1_gnn_all
    return {'x': x, 'src': src, 'dst': dst, 'L0_gnn_theta_w': _L0_gnn_in['theta_w'], 'L0_gnn_phi_w': _L0_gnn_in['phi_w'], 'L0_gnn_fc1_w': _L0_gnn_in['fc1_w'], 'L0_gnn_bn0_g': _L0_gnn_in['bn0_g'], 'L0_gnn_bn0_b': _L0_gnn_in['bn0_b'], 'L0_gnn_bn1_g': _L0_gnn_in['bn1_g'], 'L0_gnn_bn1_b': _L0_gnn_in['bn1_b'], 'L1_gnn_W1l': _L1_gnn_in['W1l'], 'L1_gnn_b1l': _L1_gnn_in['b1l'], 'L1_gnn_W1r': _L1_gnn_in['W1r'], 'L1_gnn_W2l': _L1_gnn_in['W2l'], 'L1_gnn_b2l': _L1_gnn_in['b2l'], 'L1_gnn_W2r': _L1_gnn_in['W2r']}

def reference(x, src, dst, L0_gnn_theta_w, L0_gnn_phi_w, L0_gnn_fc1_w, L0_gnn_bn0_g, L0_gnn_bn0_b, L0_gnn_bn1_g, L0_gnn_bn1_b, L1_gnn_W1l, L1_gnn_b1l, L1_gnn_W1r, L1_gnn_W2l, L1_gnn_b2l, L1_gnn_W2r):
    import jax
    import jax.numpy as jnp

    def _L0_gnn_ref(h, src, dst, theta_w, phi_w, fc1_w, bn0_g, bn0_b, bn1_g, bn1_b):
        import jax, jax.numpy as jnp
        import numpy as np
        N, E, C = (100000, 25000, 128)
        EPS = 1e-05

        def _bn(x, g, b):
            mu = jnp.mean(x, axis=0)
            var = jnp.mean((x - mu) ** 2, axis=0)
            return g * (x - mu) * jax.lax.rsqrt(var + EPS) + b
        n = h.shape[0]
        x_src = h[src]
        x_dst = h[dst]
        e = (x_dst - x_src) @ theta_w.T + x_src @ phi_w.T
        e = jax.nn.relu(_bn(e, bn0_g, bn0_b))
        e = e @ fc1_w.T
        e = jax.nn.relu(_bn(e, bn1_g, bn1_b))
        agg = jax.ops.segment_sum(e, dst, num_segments=n)
        cnt = jax.ops.segment_sum(jnp.ones((e.shape[0],), e.dtype), dst, num_segments=n)
        x = agg / jnp.maximum(cnt, 1.0)[:, None]
        return jax.nn.relu(x + h)

    def _L1_gnn_ref(x, edge_index, W1l, b1l, W1r, W2l, b2l, W2r):
        import jax, jax.numpy as jnp
        import numpy as np
        N_NODES = 100000
        N_EDGES = 25000
        D_IN = 128
        D_HID = 128
        D_OUT = 128

        def _scatter_mean(feat, src, dst, n_nodes):
            summed = jax.ops.segment_sum(feat[src], dst, num_segments=n_nodes)
            deg = jax.ops.segment_sum(jnp.ones_like(dst, dtype=feat.dtype), dst, num_segments=n_nodes)
            return summed / jnp.maximum(deg, 1.0)[:, None]

        def _sage_conv(x, src, dst, Wl, bl, Wr):
            agg = _scatter_mean(x, src, dst, x.shape[0])
            return agg @ Wl.T + bl + x @ Wr.T
        src, dst = (edge_index[0], edge_index[1])
        h = _sage_conv(x, src, dst, W1l, b1l, W1r)
        h = jax.nn.relu(h)
        out = _sage_conv(h, src, dst, W2l, b2l, W2r)
        return out
    edge_index = jnp.stack([src, dst])
    x = _layernorm(x + _L0_gnn_ref(x, src, dst, L0_gnn_theta_w, L0_gnn_phi_w, L0_gnn_fc1_w, L0_gnn_bn0_g, L0_gnn_bn0_b, L0_gnn_bn1_g, L0_gnn_bn1_b), axis=-1)
    x = _layernorm(x + _L1_gnn_ref(x, edge_index, L1_gnn_W1l, L1_gnn_b1l, L1_gnn_W1r, L1_gnn_W2l, L1_gnn_b2l, L1_gnn_W2r), axis=-1)
    return x

_drawn_inputs = setup_inputs


def setup_inputs(seed=0):
    import zlib

    import numpy as np

    out = dict(_drawn_inputs(seed))
    spreads = {'L0_gnn_bn0_g': (1.0, 0.566),
     'L0_gnn_bn0_b': (0.0, 0.707),
     'L0_gnn_bn1_g': (1.0, 0.2),
     'L0_gnn_bn1_b': (0.0, 0.577)}
    factors = {'L1_gnn_b1l': 2.905}
    for name, (base, spread) in spreads.items():
        noise = np.random.default_rng([zlib.crc32(name.encode()), seed]).standard_normal(out[name].shape)
        drawn = base * np.exp(spread * noise) if base else spread * noise
        out[name] = jnp.asarray(drawn.astype(out[name].dtype))
    for name, factor in factors.items():
        out[name] = (out[name] * factor).astype(out[name].dtype)
    return out
```

```python
import concourse.bass as bass
from concourse import mybir
from contextlib import ExitStack



def gnn_program(nc, x, src, dst, theta_w, phi_w, fc1_w, bn0_g, bn0_b, bn1_g, bn1_b,
                w1l, b1, w1r, w2l, b2, w2r, out):
    f32, i32, bf16, u8 = mybir.dt.float32, mybir.dt.int32, mybir.dt.bfloat16, mybir.dt.uint8
    ALU, ACT, AX = mybir.AluOpType, mybir.ActivationFunctionType, mybir.AxisListType
    P = 128
    N, C = x.shape
    E = src.shape[0]
    EPS = 1e-5
    T = 4
    CH = T * P
    CHUNKS = -(-E // CH)
    EP = CHUNKS * CH
    TILES = EP // P
    LASTN = E - (CHUNKS - 1) * CH
    B = 2
    Q = TILES // B
    G = 8
    UN = G * P
    UNITS = -(-N // UN)
    HALF = UN // 2
    Z = P
    PZ = 80
    assert E % P and CHUNKS % 2 == 1 and TILES == B * Q and Q <= P and N % PZ == 0 and UNITS == 2 * CHUNKS

    def scratch(name, shape, dt):
        return nc.dram_tensor(name, shape, dt, kind="Internal").ap()

    dst_pad = scratch("dst_pad", [EP + 2], i32)
    src_pad = scratch("src_pad", [EP], i32)
    same_row = scratch("same_row", [EP], u8)
    position = scratch("position", [N, 1], i32)
    xs_spill = scratch("xs_spill", [CHUNKS, P, CH], f32)
    xd_spill = scratch("xd_spill", [CHUNKS, P, CH], f32)
    mean0_tab = scratch("mean0_tab", [Z + EP, C], f32)
    t1_tab = scratch("t1_tab", [Z + EP, C], f32)
    base2 = scratch("base2", [CHUNKS, P, CH], f32)

    ctx = ExitStack()
    with ctx:
        def sb(name, shape, dt=f32):
            return ctx.enter_context(nc.sbuf_tensor(name, shape, dt))

        def pb(name, shape):
            return ctx.enter_context(nc.psum_tensor(name, shape, f32))

        def sem(name):
            return ctx.enter_context(nc.semaphore(name))

        def sems(name):
            return [sem(f"{name}{k}") for k in range(2)]

        edge_cols = sb("edge_cols", [P, EP])
        same = sb("same", [P, EP], u8)
        ident = sb("ident", [P, P])
        centre = sb("centre", [P, P])
        w_in = sb("w_in", [P, 7, P])
        thT, phT, fcT = (sb(n, [P, P]) for n in ("thT", "phT", "fcT"))
        w1lT, w1rT, w2lT, w2rT = (sb(n, [P, P]) for n in ("w1lT", "w1rT", "w2lT", "w2rT"))
        w_mean = sb("w_mean", [P, 8])
        par = sb("par", [P, 8])
        eps = sb("eps", [P, 1])
        b2_all = sb("b2_all", [P, P])
        b2_part = sb("b2_part", [P, 3, P])
        b2_bf = sb("b2_bf", [P, P], bf16)
        b2_rows = sb("b2_rows", [P, CH], bf16)
        ones_bf = sb("ones_bf", [P, P], bf16)
        ones1 = sb("ones1", [1, 1])
        inv_cnt = sb("inv_cnt", [P, TILES])
        gather1 = sb("gather1", [P, CHUNKS, 2 * T], i32)
        scat_idx = sb("scat_idx", [P, TILES], i32)
        row_of = sb("row_of", [P, TILES], i32)
        pos_idx = sb("pos_idx", [P, TILES], i32)
        lane = sb("lane", [P, T], i32)
        idx_stage = sb("idx_stage", [P, 2, 2 * T], i32)
        val_stage = sb("val_stage", [P, 2, T], i32)
        got_stage = sb("got_stage", [P, 2, T], i32)
        max_stage = sb("max_stage", [P, 2, T], i32)
        xb = sb("xb", [P, 2, UN])
        yb = sb("yb", [P, UN])
        yT = sb("yT", [P, UN])
        hT = sb("hT", [P, UN])
        sq = sb("sq", [P, UN])
        ob = sb("ob", [P, 2, UN])
        bn = sb("bn", [P, G, 6])
        small = sb("small", [P, 8, G])
        g1 = sb("g1", [P, 2, 2 * CH])
        dx = sb("dx", [P, CH])
        dT = sb("dT", [P, 2, CH])
        bnE = sb("bnE", [P, CHUNKS, 6])
        mvE = sb("mvE", [P, 8])
        rl = sb("rl", [P, 2, CH])
        sc = sb("sc", [P, 2, CH])
        tr = sb("tr", [P, 2, CH])

        PA = pb("PA", [P, UN])
        PC = pb("PC", [P, UN])
        PE_ = [pb(f"PE{k}", [P, CH]) for k in range(4)]

        def ge(e, s, v):
            if not (isinstance(v, int) and v <= 0):
                e.wait_ge(s, v)

        def wait_apart(e, s, v):
            e.wait_ge(s, v)
            e.sem_inc(s_apart, 1)

        def steps(e, first, last, body, head=2, tail=0):
            i = first
            while i < last and (i < first + head or i % 2):
                body(i, i // 2, i % 2)
                i += 1
            stop = max(i // 2, (last - tail) // 2)
            if stop > i // 2:
                with e.Fori(i // 2, stop) as j:
                    body(j * 2, j, 0)
                    body(j * 2 + 1, j, 1)
            for i in range(2 * stop if stop > i // 2 else i, last):
                body(i, i // 2, i % 2)

        def half(t, h):
            return t[:, h * HALF:(h + 1) * HALF]

        def tiles(ap, n):
            return ap.rearrange("p (t c) -> p t c", t=n)

        def cols(i):
            return bass.ds(i * CH, CH)

        s_apart = sem("waited")
        s_par, s_tlay, s_w = sem("params_loaded"), sem("targets_loaded"), sem("weights_loaded")
        s_pad, s_pads = sem("pad_tiles_set"), sem("padded_rows_written")
        s_zero, s_same, s_sameb = sem("tables_zeroed"), sem("same_row_written"), sem("same_loaded")
        s_id, s_cst = sem("identity_built"), sem("constants_set")
        s_row, s_dv, s_rowT, s_carry, s_carryT = (sem(n) for n in (
            "row_ready", "dve_setup", "row_transposed", "carry_ready", "carry_transposed"))
        s_lay, s_layT, s_idx = sem("layout_ready"), sem("layout_transposed"), sem("indices_ready")
        s_wc, s_wT, s_wR, s_b2 = (sem(n) for n in ("weights_centred", "weights_transposed", "weights_ready", "b2_ready"))
        b_x, b_st = sems("unit_loaded"), sems("unit_stored")
        b_z, b_bn, b_q = sem("z_ready"), sem("unit_stats"), sem("unit_stats_sum")
        b_var, b_std, b_r, b_y = (sem(n) for n in ("var_ready", "std_ready", "rstd_ready", "y_ready"))
        b_T, b_yT, b_w1, b_h, b_w2 = (sem(n) for n in ("y_transposed", "yT_ready", "w1_done", "h_ready", "w2_done"))
        b_sq, b_red, b_std2, b_r2, b_out = (sem(n) for n in ("squares_ready", "squares_summed", "std2_ready", "rstd2_ready", "unit_out"))
        p_idx = sem("indices_staged")
        e_g, e_sp = sems("x_rows_gathered"), sems("x_rows_spilled")
        e_dd, e_T, e_ev, e_mm, e_c, e_bn = (sem(n) for n in (
            "difference_ready", "rows_transposed", "columns_ready", "edge_product", "edge_copied", "edge_stats"))
        m_st, m_aff = sem("norm_std"), sem("norm_affine")
        f_r, f_mm, f_c = sem("relu0_ready"), sem("fc1_done"), sem("fc1_copied")
        q_set, q_get = sems("positions_set"), sems("positions_got")
        q_max = sem("positions_masked")
        k_r, k_sc, k_T, k_m = sem("relu1_ready"), sem("sum0_ready"), sem("sum0_transposed"), sem("mean0_ready")
        k_st = sems("mean0_stored")
        l_ld, l_g = sems("chunk_loaded"), sems("mean0_gathered")
        l_x, l_z, l_bn, l_q, l_var, l_std, l_r, l_y = (sem("l_" + n) for n in (
            "x1_ready", "z_ready", "stats", "stats_sum", "var_ready", "std_ready", "rstd_ready", "y_ready"))
        l_T, l_ev, l_sc, l_t, l_tu, l_h, l_hr, l_w2, l_b = (sem("l_" + n) for n in (
            "y_transposed", "y_columns", "sum1_ready", "sum1_projected", "t1_ready", "h_product", "h_ready", "w2_done", "base2_ready"))
        l_tst, l_bst = sems("t1_stored"), sems("base2_stored")
        o_g, o_b, o_st = sems("t1_gathered"), sems("base2_loaded"), sems("rows_scattered")
        o_h, o_r, o_sc, o_a, o_m, o_z, o_sq, o_red, o_std, o_rs, o_out = (sem("o_" + n) for n in (
            "h_product", "h_ready", "sum2_ready", "sum2_projected", "mean2_ready", "z_ready", "squares_ready",
            "squares_summed", "std_ready", "rstd_ready", "out_ready"))

        RL = 7
        rl_i = sq[:, :]
        def lay_i(k):
            return tiles(ob[:, k // 2, (k % 2) * HALF:(k % 2) * HALF + B * P].bitcast(i32), B)[0:Q]
        def lay(k):
            t = (xb[:, 0], xb[:, 1], yb, yT, hT)[k // 4] if k >= 8 else xb[:, k // 4]
            return tiles(t[:, (k % 4) * B * P:(k % 4) * B * P + B * P], B)[0:Q]
        START, S_, EIDX, SCAN, CNT, INV, ENDF, DM, DSC, XDI, SRCF, ONE = range(12)
        SAME8 = tiles(dT[:, 0, 0:B * P // 4].bitcast(u8), B)[0:Q]
        carry = sc[0:1, 0, 0:TILES + 1]
        row_ps = PE_[0][0:1, 0:TILES]
        carry_ps = PE_[1][0:Q, 0:B]
        lay_ps = PA

        block = ctx.enter_context(nc.Block())

        def unit_rows(t, u):
            at = N - UN if isinstance(u, int) and u == UNITS - 1 else u * UN
            return t[bass.ds(at, UN), :].rearrange("(p g) c -> p (g c)", p=P)

        def chunk_rows(tab, i):
            return tab[bass.ds(i * CH + Z, CH), :].rearrange("(t p) c -> p t c", p=P)

        @block.sync
        def _(sp):
            for k, w in enumerate((theta_w, phi_w, fc1_w, w1l, w1r, w2l, w2r)):
                sp.dma_start(w_in[:, k, :], w).then_inc(s_w, 16)
            sp.wait_ge(s_pad, 1)
            sp.dma_start(dst_pad[bass.ds(1, E)], dst).then_inc(s_pads, 16)
            sp.dma_start(src_pad[bass.ds(0, E)], src).then_inc(s_pads, 16)
            sp.dma_start(dst_pad[bass.ds(0, 1)].rearrange("(a n) -> a n", a=1), idx_stage[0:1, 0, 0:1]).then_inc(s_pads, 16)
            sp.dma_start(dst_pad[bass.ds(1 + E, EP + 1 - E)].rearrange("(a n) -> a n", a=1),
                         pos_idx[0:1, 0:EP + 1 - E]).then_inc(s_pads, 16)
            sp.dma_start(src_pad[bass.ds(E, EP - E)].rearrange("(a n) -> a n", a=1),
                         row_of[0:1, 0:EP - E]).then_inc(s_pads, 16)
            sp.wait_ge(s_pads, 80)
            for k in range(3):
                sp.dma_start(lay_i(k), dst_pad[bass.ds(k, EP)].rearrange("(b q n) -> q b n", b=B, q=Q)).then_inc(s_tlay, 16)
            sp.dma_start(lay_i(3), src_pad.rearrange("(b q n) -> q b n", b=B, q=Q)).then_inc(s_tlay, 16)
            for k, v in enumerate((bn0_g, bn0_b, bn1_g, bn1_b, b1)):
                sp.dma_start(par[:, k:k + 1], v.rearrange("(p a) -> p a", a=1)).then_inc(s_par, 16)
            sp.dma_start(b2_all[:, :], b2.rearrange("(a n) -> a n", a=1).to_broadcast([P, C])).then_inc(s_par, 16)
            sp.wait_ge(s_same, 1)
            sp.dma_start(same_row.rearrange("(b q n) -> q b n", b=B, q=Q), SAME8).then_inc(s_sameb, 16)
            sp.wait_ge(s_sameb, 16)
            sp.dma_start(same[:, :], same_row.rearrange("(a n) -> a n", a=1).to_broadcast([P, EP])).then_inc(s_sameb, 16)
            sp.dma_start(position.rearrange("(p n) a -> p (n a)", p=PZ),
                         edge_cols[0:PZ, 0:N // PZ].bitcast(i32)).then_inc(s_zero, 16)
            sp.dma_start(mean0_tab[0:Z, :], edge_cols[:, 0:C]).then_inc(s_zero, 16)
            sp.dma_start(t1_tab[0:Z, :], edge_cols[:, 0:C]).then_inc(s_zero, 16)
            sp.wait_ge(s_idx, 1)
            def load_unit(u, j, p):
                ge(sp, b_y, u - 1)
                sp.dma_start(xb[:, p, :], unit_rows(x, u)).then_inc(b_x[p], 16)

            def store_unit(u, j, p):
                ge(sp, b_out, u + 1)
                if isinstance(u, int) and u == UNITS - 1:
                    sp.wait_ge(b_st[1 - p], 16 * (j + 1))
                sp.dma_start(unit_rows(out, u), ob[:, p, :]).then_inc(b_st[p], 16)

            def edge1(i, j, p):
                load_unit(i, j, p)
                sp.wait_ge(e_g[p], 128 * (j + 1))
                sp.dma_start(xs_spill[i] if isinstance(i, int) else xs_spill[bass.ds(i, 1)].rearrange("a p n -> (a p) n"),
                             g1[:, p, 0:CH]).then_inc(e_sp[p], 16)
                sp.dma_start(xd_spill[i] if isinstance(i, int) else xd_spill[bass.ds(i, 1)].rearrange("a p n -> (a p) n"),
                             g1[:, p, CH:2 * CH]).then_inc(e_sp[p], 16)
                if isinstance(i, int) and i == 0:
                    return
                store_unit(i - 1, *((i - 1) // 2, 1 - p) if isinstance(i, int) else (j - 1 + p, 1 - p))
            steps(sp, 0, CHUNKS, edge1)

            def store_mean0(i, j, p):
                sp.wait_ge(k_m, i + 1)
                sp.dma_start(chunk_rows(mean0_tab, i), tiles(tr[:, p, :], T)).then_inc(k_st[p], 16)
            steps(sp, 0, CHUNKS, store_mean0)

            def dense(u, j, p):
                load_unit(u, j, p)
                store_unit(u - 1, *((u - 1) // 2, 1 - p) if isinstance(u, int) else (j - 1 + p, 1 - p))
            steps(sp, CHUNKS, UNITS, dense, tail=2)
            store_unit(UNITS - 1, (UNITS - 1) // 2, (UNITS - 1) % 2)
            sp.wait_ge(k_st[0], 16 * ((CHUNKS + 1) // 2))
            sp.wait_ge(k_st[1], 16 * (CHUNKS // 2))
            sp.wait_ge(e_sp[0], 32 * ((CHUNKS + 1) // 2))
            sp.wait_ge(e_sp[1], 32 * (CHUNKS // 2))
            sp.wait_ge(b_y, UNITS)

            def at(t, i):
                return t[i] if isinstance(i, int) else t[bass.ds(i, 1)].rearrange("a p n -> (a p) n")

            def load5(i, j, p):
                ge(sp, l_x, i - 1)
                sp.dma_start(xb[:, p, 0:CH], at(xs_spill, i)).then_inc(l_ld[p], 16)
                sp.dma_start(xb[:, p, CH:2 * CH], at(xd_spill, i)).then_inc(l_ld[p], 16)
                sp.dma_start(tiles(ob[:, p, CH:2 * CH], T), chunk_rows(mean0_tab, i)).then_inc(l_ld[p], 16)

            def store5(i, j, p):
                sp.wait_ge(l_tu, i + 1)
                sp.dma_start(chunk_rows(t1_tab, i), tiles(tr[:, p, :], T)).then_inc(l_tst[p], 16)
                sp.wait_ge(l_b, i + 1)
                sp.dma_start(at(base2, i), rl[:, p, :]).then_inc(l_bst[p], 16)

            def edge5(i, j, p):
                load5(i, j, p)
                if not (isinstance(i, int) and i == 0):
                    store5(i - 1, *((i - 1) // 2, 1 - p) if isinstance(i, int) else (j - 1 + p, 1 - p))
            steps(sp, 0, CHUNKS, edge5)
            store5(CHUNKS - 1, (CHUNKS - 1) // 2, (CHUNKS - 1) % 2)
            sp.wait_ge(l_bst[0], 16 * ((CHUNKS + 1) // 2))
            sp.wait_ge(l_bst[1], 16 * (CHUNKS // 2))
            sp.wait_ge(l_y, CHUNKS)

            def load6(i, j, p):
                ge(sp, o_z, i - 1)
                sp.dma_start(xb[:, p, 0:CH], at(base2, i)).then_inc(o_b[p], 16)
            steps(sp, 0, CHUNKS, load6)

        @block.gpsimd
        def _(gp):
            gp.memset(ident[:, :], 0.0).then_inc(s_id, 1)
            gp.wait_ge(s_id, 1)
            gp.affine_select(out=ident[:, :], in_=ident[:, :], compare_op=ALU.not_equal, fill=1.0,
                             base=0, pattern=[[-1, P]], channel_multiplier=1).then_inc(s_id, 1)
            gp.iota(lay(EIDX), [[Q * P, B], [1, P]], base=0, channel_multiplier=P,
                    allow_small_or_imprecise_dtypes=True).then_inc(s_id, 1)
            gp.iota(lane[:, :], [[0, T]], base=0, channel_multiplier=1).then_inc(s_id, 1)
            gp.wait_ge(s_pads, 80)
            gp.iota(row_of[:, :], [[P, TILES]], base=Z, channel_multiplier=1).then_inc(s_id, 1)
            gp.wait_ge(s_id, 5)
            gp.wait_ge(s_idx, 1)

            def rows(i, j, p):
                ge(gp, e_sp[p], 32 * j)
                ge(gp, e_dd, i - 1)
                ge(gp, e_T, i - 1)
                gp.tensor_copy(idx_stage[:, p, :], gather1[:, i, :] if isinstance(i, int)
                               else gather1[:, bass.ds(i, 1), :].rearrange("p a n -> p (a n)")).then_inc(p_idx, 1)
                wait_apart(gp, p_idx, i + 1)
                for t in range(2 * T):
                    gp.indirect_dma_start(g1[:, p, t * C:(t + 1) * C], None, x,
                                          bass.IndirectOffsetOnAxis(ap=idx_stage[:, p, t:t + 1], axis=0)).then_inc(e_g[p], 16)
            steps(gp, 0, CHUNKS, rows)

            gp.wait_ge(s_zero, 48)
            P1 = CHUNKS
            def set_pos(i, j, p):
                ge(gp, q_set[p], 64 * j)
                gp.tensor_copy(idx_stage[:, p, 0:T], scat_idx[:, bass.ds(i * T, T)]).then_inc(p_idx, 1)
                gp.tensor_copy(val_stage[:, p, :], row_of[:, bass.ds(i * T, T)]).then_inc(p_idx, 1)
                wait_apart(gp, p_idx, P1 + 2 * i + 2)
                for t in range(T):
                    gp.indirect_dma_start(position, bass.IndirectOffsetOnAxis(ap=idx_stage[:, p, t:t + 1], axis=0),
                                          val_stage[:, p, t:t + 1], None, bounds_check=N - 1, oob_is_err=False).then_inc(q_set[p], 16)
            gp.wait_ge(e_g[0], 128 * ((CHUNKS + 1) // 2))
            gp.wait_ge(e_g[1], 128 * (CHUNKS // 2))
            steps(gp, 0, CHUNKS, set_pos)
            gp.wait_ge(q_set[0], 64 * ((CHUNKS + 1) // 2))
            gp.wait_ge(q_set[1], 64 * (CHUNKS // 2))

            P2 = 3 * CHUNKS
            def mask_pos(i, j, p):
                wait_apart(gp, q_get[p], 64 * (j + 1))
                gp.tensor_scalar(max_stage[:, p, :], got_stage[:, p, :], lane[:, 0:1], None, ALU.max).then_inc(q_max, 1)
                wait_apart(gp, q_max, 2 * i + 1)
                gp.tensor_copy(pos_idx[:, bass.ds(i * T, T)], max_stage[:, p, :]).then_inc(q_max, 1)

            def get_pos(i, j, p):
                ge(gp, q_max, 2 * i - 2)
                gp.tensor_copy(idx_stage[:, p, 0:T], gather1[:, i, 0:T] if isinstance(i, int)
                               else gather1[:, bass.ds(i, 1), 0:T].rearrange("p a n -> p (a n)")).then_inc(p_idx, 1)
                wait_apart(gp, p_idx, P2 + i + 1)
                for t in range(T):
                    gp.indirect_dma_start(got_stage[:, p, t:t + 1], None, position,
                                          bass.IndirectOffsetOnAxis(ap=idx_stage[:, p, t:t + 1], axis=0)).then_inc(q_get[p], 16)
                if not (isinstance(i, int) and i == 0):
                    mask_pos(i - 1, *((i - 1) // 2, 1 - p) if isinstance(i, int) else (j - 1 + p, 1 - p))
            steps(gp, 0, CHUNKS, get_pos)
            mask_pos(CHUNKS - 1, (CHUNKS - 1) // 2, (CHUNKS - 1) % 2)
            wait_apart(gp, q_max, 2 * CHUNKS)

            gp.wait_ge(k_st[0], 16 * ((CHUNKS + 1) // 2))
            gp.wait_ge(k_st[1], 16 * (CHUNKS // 2))
            gp.wait_ge(b_st[0], 16 * (UNITS // 2))
            gp.wait_ge(b_st[1], 16 * (UNITS // 2))
            P3 = 4 * CHUNKS
            def gather5(i, j, p):
                ge(gp, l_x, i - 1)
                gp.tensor_copy(idx_stage[:, p, 0:T], pos_idx[:, bass.ds(i * T, T)]).then_inc(p_idx, 1)
                wait_apart(gp, p_idx, P3 + i + 1)
                for t in range(T):
                    gp.indirect_dma_start(ob[:, p, t * C:(t + 1) * C], None, mean0_tab,
                                          bass.IndirectOffsetOnAxis(ap=idx_stage[:, p, t:t + 1], axis=0)).then_inc(l_g[p], 16)
            steps(gp, 0, CHUNKS, gather5)

            gp.wait_ge(l_tst[0], 16 * ((CHUNKS + 1) // 2))
            gp.wait_ge(l_tst[1], 16 * (CHUNKS // 2))
            P4 = 5 * CHUNKS
            def gather6(i, j, p):
                ge(gp, o_h, i - 1)
                gp.tensor_copy(idx_stage[:, p, 0:T], pos_idx[:, bass.ds(i * T, T)]).then_inc(p_idx, 1)
                if isinstance(i, int) and i < 2:
                    wait_apart(gp, p_idx, P4 + i + 1)
                else:
                    wait_apart(gp, p_idx, P4 + 2 * i - 1)
                for t in range(T):
                    gp.indirect_dma_start(g1[:, p, t * C:(t + 1) * C], None, t1_tab,
                                          bass.IndirectOffsetOnAxis(ap=idx_stage[:, p, t:t + 1], axis=0)).then_inc(o_g[p], 16)

            def scatter6(i, j, p):
                ge(gp, o_st[p], 64 * j)
                gp.wait_ge(o_out, i + 1)
                gp.tensor_copy(idx_stage[:, p, T:2 * T], scat_idx[:, bass.ds(i * T, T)]).then_inc(p_idx, 1)
                wait_apart(gp, p_idx, P4 + 2 * CHUNKS - 1 + i - (CHUNKS - 2) if isinstance(i, int) and i >= CHUNKS - 2 else P4 + 2 * i + 4)
                for t in range(T):
                    gp.indirect_dma_start(out, bass.IndirectOffsetOnAxis(ap=idx_stage[:, p, T + t:T + t + 1], axis=0),
                                          ob[:, p, t * C:(t + 1) * C], None, bounds_check=N - 1, oob_is_err=False).then_inc(o_st[p], 16)
            gather6(0, 0, 0)
            gather6(1, 0, 1)

            def turn6(i, j, p):
                gather6(i, j, p)
                scatter6(i - 2, j - 1, p)
            steps(gp, 2, CHUNKS, turn6, head=0)
            scatter6(CHUNKS - 2, (CHUNKS - 2) // 2, (CHUNKS - 2) % 2)
            scatter6(CHUNKS - 1, (CHUNKS - 1) // 2, (CHUNKS - 1) % 2)
            gp.wait_ge(o_st[0], 64 * ((CHUNKS + 1) // 2))
            gp.wait_ge(o_st[1], 64 * (CHUNKS // 2))
            gp.wait_ge(s_zero, 48)

        def prev(i, j, p):
            return (i - 1, (i - 1) // 2, 1 - p) if isinstance(i, int) else (i - 1, j - 1 + p, 1 - p)

        @block.scalar
        def _(act):
            def root(o, i, s, e):
                return act.activation(o, i, ACT.Sqrt, bias=eps[:, 0:1], scale=s)

            def unit_front(u, j, p):
                act.wait_ge(b_var, u + 1)
                root(small[:, 3, :], small[:, 2, :], 1.0 / C, EPS).then_inc(b_std, 1)
                first = isinstance(u, int) and u == 0
                if not first:
                    unit_squares(*prev(u, j, p))

            def unit_squares(u, j, p):
                act.wait_ge(b_w2, 2 * u + 2)
                ge(act, b_red, u)
                act.activation(sq[:, :], PC[:, :], ACT.Square).then_inc(b_sq, 1)

            def unit_root2(u, j, p):
                act.wait_ge(b_red, u + 1)
                root(small[:, 6, :], small[:, 5, :], 1.0 / C, EPS).then_inc(b_std2, 1)

            def unit_back(u, j, p):
                for h in range(2):
                    act.wait_ge(b_T, 2 * u + 1 + h)
                    ge(act, b_w2, 2 * u - 1 + h)
                    act.activation(half(yT, h), half(PA, h), ACT.Copy).then_inc(b_yT, 1)
                if not (isinstance(u, int) and u == 0):
                    unit_root2(*prev(u, j, p))
                for h in range(2):
                    act.wait_ge(b_w1, 2 * u + 1 + h)
                    act.activation(half(hT, h), half(PA, h), ACT.Relu, bias=par[:, 4:5]).then_inc(b_h, 1)

            act.wait_ge(s_cst, 1)
            act.wait_ge(s_wT, 1)
            act.wait_ge(s_wR, 2)
            act.activation(thT[:, :], PE_[2][:, 0:P], ACT.Copy).then_inc(s_wR, 1)
            act.activation(phT[:, :], PE_[2][:, P:2 * P], ACT.Copy).then_inc(s_wR, 1)
            act.activation(fcT[:, :], PE_[2][:, 2 * P:3 * P], ACT.Copy).then_inc(s_wR, 1)
            act.activation(w1lT[:, :], PE_[2][:, 3 * P:4 * P], ACT.Copy).then_inc(s_wR, 1)
            act.activation(w1rT[:, :], PE_[3][:, 0:P], ACT.Copy).then_inc(s_wR, 1)
            act.wait_ge(s_par, 96)
            act.wait_ge(s_sameb, 32)
            act.wait_ge(s_zero, 48)

            def edge1(i, j, p):
                act.wait_ge(e_T, i + 1)
                ge(act, e_mm, i)
                act.activation(dT[:, 0, :], PE_[0][:, :], ACT.Copy).then_inc(e_ev, 1)
                act.activation(dT[:, 1, :], PE_[1][:, :], ACT.Copy).then_inc(e_ev, 1)
                unit_front(i, j, p)
                act.wait_ge(e_mm, i + 1)
                act.activation(edge_cols[:, cols(i)], PE_[2][:, :], ACT.Copy).then_inc(e_c, 1)
                unit_back(i, j, p)
            steps(act, 0, CHUNKS, edge1)

            act.wait_ge(m_aff, 1)
            act.activation(mvE[:, 2:3], mvE[:, 1:2], ACT.Sqrt, bias=eps[:, 0:1]).then_inc(m_st, 1)
            act.wait_ge(m_aff, 3)

            def edge2(i, j, p):
                ge(act, f_mm, i - 1)
                act.activation(rl[:, p, :], edge_cols[:, cols(i)], ACT.Relu, bias=mvE[:, 4:5], scale=mvE[:, 3:4]).then_inc(f_r, 1)
            steps(act, 0, CHUNKS, edge2)
            act.wait_ge(m_aff, 4)
            act.activation(mvE[:, 2:3], mvE[:, 1:2], ACT.Sqrt, bias=eps[:, 0:1]).then_inc(m_st, 1)
            act.wait_ge(m_aff, 6)

            def edge3(i, j, p):
                ge(act, k_sc, i - 1)
                act.activation(rl[:, p, :], edge_cols[:, cols(i)], ACT.Relu, bias=mvE[:, 4:5], scale=mvE[:, 3:4]).then_inc(k_r, 1)
            steps(act, 0, CHUNKS, edge3)

            def dense(u, j, p):
                unit_front(u, j, p)
                unit_back(u, j, p)
            steps(act, CHUNKS, UNITS, dense)
            last = (UNITS - 1, (UNITS - 1) // 2, (UNITS - 1) % 2)
            unit_squares(*last)
            unit_root2(*last)

            def h5(i, j, p):
                act.wait_ge(l_h, i + 1)
                act.activation(dT[:, 0, :], PE_[1][:, :], ACT.Relu, bias=par[:, 4:5]).then_inc(l_hr, 1)
                act.wait_ge(l_w2, i + 1)
                ge(act, l_bst[p], 16 * j)
                act.activation(rl[:, p, :], PE_[2][:, :], ACT.Copy).then_inc(l_b, 1)

            def edge5(i, j, p):
                act.wait_ge(l_var, i + 1)
                root(small[:, 3, :], small[:, 2, :], 1.0 / C, EPS).then_inc(l_std, 1)
                act.wait_ge(l_T, 2 * i + 1)
                act.activation(edge_cols[:, cols(i)], half(PA, 0), ACT.Copy).then_inc(l_ev, 1)
                act.wait_ge(l_T, 2 * i + 2)
                ge(act, l_w2, i - 1)
                act.activation(half(yT, p), half(PA, 1), ACT.Copy).then_inc(l_ev, 1)
                if not (isinstance(i, int) and i == 0):
                    h5(*prev(i, j, p))
            steps(act, 0, CHUNKS, edge5)
            h5(CHUNKS - 1, (CHUNKS - 1) // 2, (CHUNKS - 1) % 2)

            def root6(i, j, p):
                act.wait_ge(o_red, i + 1)
                root(small[:, 6, 0:T], small[:, 5, 0:T], 1.0 / C, EPS).then_inc(o_std, 1)

            def edge6(i, j, p):
                act.wait_ge(o_h, i + 1)
                ge(act, o_sc, i - 1)
                act.activation(rl[:, p, :], PE_[0][:, :], ACT.Relu, bias=par[:, 4:5]).then_inc(o_r, 1)
                if not (isinstance(i, int) and i == 0):
                    root6(*prev(i, j, p))
                act.wait_ge(o_z, i + 1)
                act.activation(half(sq, p), tr[:, p, :], ACT.Square).then_inc(o_sq, 1)
            act.wait_ge(l_bst[0], 16 * ((CHUNKS + 1) // 2))
            act.wait_ge(l_bst[1], 16 * (CHUNKS // 2))
            steps(act, 0, CHUNKS, edge6)
            root6(CHUNKS - 1, (CHUNKS - 1) // 2, (CHUNKS - 1) % 2)

        @block.tensor
        def _(pe):
            pe.wait_ge(s_id, 2)
            pe.wait_ge(s_cst, 1)
            pe.wait_ge(s_row, 1)
            for b in range(B):
                last = pe.matmul(row_ps[:, b * Q:(b + 1) * Q], lay(SCAN)[:, b, P - 1:P], ident[0:Q, 0:Q], start=True, stop=True)
            last.then_inc(s_rowT, 1)
            pe.wait_ge(s_carry, 1)
            for b in range(B):
                last = pe.matmul(carry_ps[:, b:b + 1], carry[:, b * Q:(b + 1) * Q], ones1[:, :], start=True, stop=True)
            last.then_inc(s_carryT, 1)
            pe.wait_ge(s_lay, 1)
            for k, row in enumerate((INV, DSC, XDI, SRCF)):
                for b in range(B):
                    at = (k // 2) * HALF + ((k % 2) * B + b) * Q
                    last = pe.transpose(lay_ps[:, at:at + Q], lay(row)[:, b, :], ident[0:Q, 0:Q])
            last.then_inc(s_layT, 1)
            pe.wait_ge(s_wc, 1)
            for k, w in enumerate((0, 1, 2, 3, 4, 5, 6)):
                last = pe.transpose(PE_[2 + k // 4][:, (k % 4) * P:(k % 4 + 1) * P], w_in[:, w, :], ident[:, :])
            last.then_inc(s_wT, 1)
            pe.wait_ge(s_wR, 7)
            pe.wait_ge(s_b2, 1)
            pe.wait_ge(s_idx, 1)

            def unit(u, j, p):
                pe.wait_ge(b_y, u + 1)
                for h in range(2):
                    ge(pe, b_h, 2 * u - 1 + h)
                    for t in range(4 * h, 4 * h + 4):
                        last = pe.transpose(PA[:, t * P:(t + 1) * P], yb[:, t * P:(t + 1) * P], ident[:, :])
                    last.then_inc(b_T, 1)
                for h in range(2):
                    pe.wait_ge(b_yT, 2 * u + 1 + h)
                    pe.matmul(half(PA, h), w1rT[:, :], half(yT, h), start=True, stop=True).then_inc(b_w1, 1)
                ge(pe, b_out, u)
                for h in range(2):
                    pe.wait_ge(b_h, 2 * u + 1 + h)
                    pe.matmul(half(PC, h), ones_bf[:, :], b2_rows[:, :], start=True, stop=False)
                    for t in range(4 * h, 4 * h + 4):
                        o = PC[:, t * P:(t + 1) * P]
                        pe.matmul(o, hT[:, t * P:(t + 1) * P], w2rT[:, :], start=False, stop=False)
                        last = pe.matmul(o, yT[:, t * P:(t + 1) * P], centre[:, :], start=False, stop=t % 4 == 3)
                    last.then_inc(b_w2, 1)

            def edge1(i, j, p):
                pe.wait_ge(e_dd, i + 1)
                for t in range(T):
                    pe.transpose(PE_[0][:, t * P:(t + 1) * P], dx[:, t * C:(t + 1) * C], ident[:, :])
                for t in range(T):
                    last = pe.transpose(PE_[1][:, t * P:(t + 1) * P], g1[:, p, t * C:(t + 1) * C], ident[:, :])
                last.then_inc(e_T, 1)
                pe.wait_ge(e_ev, 2 * i + 2)
                ge(pe, e_c, i)
                pe.matmul(PE_[2][:, :], thT[:, :], dT[:, 0, :], start=True, stop=False)
                pe.matmul(PE_[2][:, :], phT[:, :], dT[:, 1, :], start=False, stop=True).then_inc(e_mm, 1)
                unit(i, j, p)
            steps(pe, 0, CHUNKS, edge1)

            def edge2(i, j, p):
                pe.wait_ge(f_r, i + 1)
                ge(pe, f_c, i - 1)
                pe.matmul(PE_[p][:, :], fcT[:, :], rl[:, p, :], start=True, stop=True).then_inc(f_mm, 1)
            steps(pe, 0, CHUNKS, edge2)

            def edge3(i, j, p):
                pe.wait_ge(k_sc, i + 1)
                ge(pe, k_m, i - 1)
                for t in range(T):
                    last = pe.transpose(PE_[p][:, t * P:(t + 1) * P], sc[:, p, t * P:(t + 1) * P], ident[:, :])
                last.then_inc(k_T, 1)
            steps(pe, 0, CHUNKS, edge3)
            steps(pe, CHUNKS, UNITS, unit)

            def tail5(i, j, p):
                pe.wait_ge(l_tu, i + 1)
                ge(pe, l_hr, i)
                pe.matmul(PE_[1][:, :], w1rT[:, :], half(yT, p), start=True, stop=False)
                for t in range(T):
                    last = pe.matmul(PE_[1][:, t * P:(t + 1) * P], tr[:, p, t * C:(t + 1) * C], ident[:, :], start=False, stop=t == T - 1)
                last.then_inc(l_h, 1)
                pe.wait_ge(l_hr, i + 1)
                ge(pe, l_b, i)
                pe.matmul(PE_[2][:, :], ones_bf[:, :], b2_rows[:, :], start=True, stop=False)
                for t in range(T):
                    o = PE_[2][:, t * P:(t + 1) * P]
                    pe.matmul(o, dT[:, 0, t * P:(t + 1) * P], w2rT[:, :], start=False, stop=False)
                    last = pe.matmul(o, yT[:, p * CH + t * P:p * CH + (t + 1) * P], centre[:, :], start=False, stop=t == T - 1)
                last.then_inc(l_w2, 1)

            def project5(i, j, p):
                pe.wait_ge(l_sc, i + 1)
                ge(pe, l_tu, i)
                for t in range(T):
                    last = pe.matmul(PE_[0][:, t * C:(t + 1) * C], sc[:, p, t * P:(t + 1) * P], w1lT[:, :], start=True, stop=True)
                last.then_inc(l_t, 1)

            def edge5(i, j, p):
                first = isinstance(i, int) and i == 0
                if not first:
                    project5(*prev(i, j, p))
                pe.wait_ge(l_y, i + 1)
                ge(pe, l_sc, i)
                ge(pe, l_ev, 2 * i)
                for h in range(2):
                    for t in range(4 * h, 4 * h + 4):
                        last = pe.transpose(PA[:, t * P:(t + 1) * P], yb[:, t * P:(t + 1) * P], ident[:, :])
                    last.then_inc(l_T, 1)
                if not first:
                    tail5(*prev(i, j, p))
            steps(pe, 0, CHUNKS, edge5)
            end = (CHUNKS - 1, (CHUNKS - 1) // 2, (CHUNKS - 1) % 2)
            project5(*end)
            tail5(*end)

            def edge6(i, j, p):
                pe.wait_ge(o_g[p], 64 * (j + 1))
                ge(pe, o_r, i)
                pe.matmul(PE_[0][:, :], w1rT[:, :], edge_cols[:, cols(i)], start=True, stop=False)
                for t in range(T):
                    last = pe.matmul(PE_[0][:, t * P:(t + 1) * P], g1[:, p, t * C:(t + 1) * C], ident[:, :], start=False, stop=t == T - 1)
                last.then_inc(o_h, 1)
                pe.wait_ge(o_sc, i + 1)
                ge(pe, o_m, i)
                for t in range(T):
                    last = pe.matmul(PE_[1][:, t * C:(t + 1) * C], sc[:, p, t * P:(t + 1) * P], w2lT[:, :], start=True, stop=True)
                last.then_inc(o_a, 1)
            steps(pe, 0, CHUNKS, edge6)

        @block.vector
        def _(dve):
            n = [0]

            def link(ins):
                n[0] += 1
                ins.then_inc(s_dv, 1)
                dve.wait_ge(s_dv, n[0])

            dve.memset(idx_stage[:, :, :], -1)
            dve.memset(row_of[:, :], 0)
            dve.memset(pos_idx[:, :], N).then_inc(s_pad, 1)
            link(dve.memset(edge_cols[:, 0:N // PZ], 0.0))
            dve.memset(lay(ONE), 1.0)
            dve.memset(ones_bf[:, :], 1.0)
            dve.memset(ones1[:, :], 1.0)
            dve.memset(carry[:, 0:1], 0.0)
            dve.memset(eps[:, :], EPS).then_inc(s_cst, 1)
            dve.wait_ge(s_cst, 1)
            dve.wait_ge(s_tlay, 64)
            dve.tensor_tensor(SAME8, lay_i(1), lay_i(0), ALU.is_equal).then_inc(s_same, 1)
            dve.tensor_tensor(lay(START), lay_i(1), lay_i(0), ALU.not_equal)
            dve.tensor_tensor(lay(ENDF), lay_i(1), lay_i(2), ALU.not_equal)
            dve.tensor_scalar(lay(DM), lay_i(1), float(-N), None, ALU.add)
            dve.tensor_scalar(lay(XDI), lay_i(1), float(N - 1), None, ALU.min)
            link(dve.tensor_copy(lay(SRCF), lay_i(3)))
            dve.wait_ge(s_id, 3)
            link(dve.tensor_tensor(lay(S_), lay(START), lay(EIDX), ALU.mult))
            for b in range(B):
                last = dve.tensor_tensor_scan(lay(SCAN)[:, b, :], lay(ONE)[:, b, :], lay(S_)[:, b, :], 0.0, ALU.mult, ALU.max)
            last.then_inc(s_row, 1)
            link(dve.tensor_tensor(lay(DM), lay(DM), lay(ENDF), ALU.mult))
            link(dve.tensor_scalar(lay(DSC), lay(DM), float(N), None, ALU.add))
            dve.wait_ge(s_rowT, 1)
            link(dve.memset(sc[0:1, 1, 0:TILES], 1.0))
            dve.tensor_tensor_scan(carry[:, 1:TILES + 1], sc[0:1, 1, 0:TILES], row_ps, 0.0, ALU.mult, ALU.max).then_inc(s_carry, 1)
            dve.wait_ge(s_carryT, 1)
            for b in range(B):
                last = dve.tensor_scalar(lay(CNT)[:, b, :], lay(SCAN)[:, b, :], carry_ps[:, b:b + 1], -1.0, ALU.max, ALU.add)
            link(last)
            link(dve.tensor_tensor(lay(CNT), lay(EIDX), lay(CNT), ALU.subtract))
            dve.reciprocal(lay(INV), lay(CNT)).then_inc(s_lay, 1)
            dve.wait_ge(s_layT, 1)
            def col(k):
                at = (k // 2) * HALF + (k % 2) * TILES
                return lay_ps[:, at:at + TILES]
            dve.tensor_copy(inv_cnt[:, :], col(0))
            dve.tensor_copy(scat_idx[:, :], col(1))
            dve.tensor_copy(gather1[:, :, T:2 * T], col(2).rearrange("p (n t) -> p n t", t=T))
            dve.tensor_copy(gather1[:, :, 0:T], col(3).rearrange("p (n t) -> p n t", t=T)).then_inc(s_idx, 1)
            dve.wait_ge(s_w, 112)
            dve.wait_ge(s_idx, 1)
            dve.tensor_scalar(centre[:, :], ident[:, :], -1.0 / C, None, ALU.add)
            link(dve.tensor_reduce(w_mean[:, 0:2], w_in[:, 3:5, :], AX.X, ALU.add))
            link(dve.tensor_scalar(w_mean[:, 2:4], w_mean[:, 0:2], -1.0 / C, None, ALU.mult))
            dve.tensor_tensor(w_in[:, 3:5, :], w_in[:, 3:5, :], w_mean[:, 2:4].unsqueeze(2).to_broadcast([P, 2, P]), ALU.add).then_inc(s_wc, 1)
            dve.wait_ge(s_wT, 1)
            w2 = PE_[3][:, P:3 * P].rearrange("p (a c) -> p a c", a=2)
            link(dve.tensor_reduce(w_mean[:, 4:6], w2, AX.X, ALU.add))
            link(dve.tensor_scalar(w_mean[:, 6:8], w_mean[:, 4:6], -1.0 / C, None, ALU.mult))
            dve.tensor_scalar(w2lT[:, :], PE_[3][:, P:2 * P], w_mean[:, 6:7], None, ALU.add)
            dve.tensor_scalar(w2rT[:, :], PE_[3][:, 2 * P:3 * P], w_mean[:, 7:8], None, ALU.add).then_inc(s_wR, 2)
            dve.wait_ge(s_par, 96)
            link(dve.tensor_reduce(w_mean[:, 0:1], b2_all[:, :], AX.X, ALU.add))
            link(dve.tensor_scalar(w_mean[:, 1:2], w_mean[:, 0:1], -1.0 / C, None, ALU.mult))
            link(dve.tensor_scalar(b2_all[:, :], b2_all[:, :], w_mean[:, 1:2], None, ALU.add))
            for k in range(3):
                link(dve.tensor_copy(b2_bf[:, :], b2_all[:, :]))
                link(dve.tensor_copy(b2_part[:, k, :], b2_bf[:, :]))
                link(dve.tensor_tensor(b2_all[:, :], b2_all[:, :], b2_part[:, k, :], ALU.subtract))
            link(dve.tensor_scalar(b2_part[:, 0, :], b2_part[:, 0, :], ident[:, 0:1], None, ALU.mult))
            for k in (1, 2):
                link(dve.scalar_tensor_tensor(b2_part[:, 0, :], b2_part[:, k, :], ident[:, k:k + 1], b2_part[:, 0, :], ALU.mult, ALU.add))
            dve.tensor_copy(b2_rows[:, :].rearrange("p (a c) -> p a c", a=4),
                            b2_part[:, 0:1, :].to_broadcast([P, 4, P])).then_inc(s_b2, 1)

            def spread(v, k):
                return v.unsqueeze(2).to_broadcast([P, k, C])

            def moments(z, k, s_bn, s_q, s_var, i):
                for t in range(k):
                    last = dve.bn_stats(bn[:, t, :], z[:, t * C:(t + 1) * C])
                last.then_inc(s_bn, 1)
                dve.wait_ge(s_bn, i + 1)
                dve.tensor_tensor(small[:, 0, 0:k], bn[:, 0:k, 1], bn[:, 0:k, 4], ALU.subtract)
                dve.tensor_tensor(small[:, 1, 0:k], bn[:, 0:k, 2], bn[:, 0:k, 5], ALU.add).then_inc(s_q, 1)
                dve.wait_ge(s_q, 2 * i + 1)
                dve.scalar_tensor_tensor(small[:, 4, 0:k], small[:, 0, 0:k], C / 4.0, small[:, 0, 0:k], ALU.mult, ALU.mult).then_inc(s_q, 1)
                dve.wait_ge(s_q, 2 * i + 2)
                dve.tensor_tensor(small[:, 2, 0:k], small[:, 4, 0:k], small[:, 1, 0:k], ALU.add).then_inc(s_var, 1)

            def unit_a(u, j, p):
                dve.wait_ge(b_x[p], 16 * (j + 1))
                dve.scalar_tensor_tensor(xb[:, p, :], xb[:, p, :], 0.0, xb[:, p, :], ALU.max, ALU.add).then_inc(b_z, 1)
                dve.wait_ge(b_z, u + 1)
                moments(xb[:, p, :], G, b_bn, b_q, b_var, u)

            def unit_b(u, j, p):
                dve.wait_ge(b_std, u + 1)
                dve.reciprocal(small[:, 7, :], small[:, 3, :]).then_inc(b_r, 1)
                ge(dve, b_T, 2 * u)
                dve.wait_ge(b_r, u + 1)
                dve.tensor_tensor(tiles(yb[:, :], G), tiles(xb[:, p, :], G), spread(small[:, 7, :], G), ALU.mult).then_inc(b_y, 1)

            def unit_c(u, j, p):
                dve.wait_ge(b_sq, u + 1)
                dve.tensor_reduce(small[:, 5, :], tiles(sq[:, :], G), AX.X, ALU.add).then_inc(b_red, 1)
                dve.wait_ge(b_std2, u + 1)
                dve.reciprocal(small[:, 0, :], small[:, 6, :]).then_inc(b_r2, 1)
                ge(dve, b_st[p], 16 * j)
                dve.wait_ge(b_r2, u + 1)
                dve.tensor_tensor(tiles(ob[:, p, :], G), tiles(PC[:, :], G), spread(small[:, 0, :], G), ALU.mult).then_inc(b_out, 1)

            def edge1(i, j, p):
                dve.wait_ge(e_g[p], 128 * (j + 1))
                ge(dve, e_T, i)
                dve.tensor_tensor(dx[:, :], g1[:, p, CH:2 * CH], g1[:, p, 0:CH], ALU.subtract).then_inc(e_dd, 1)
                unit_a(i, j, p)
                unit_b(i, j, p)
                dve.wait_ge(e_c, i + 1)
                end = isinstance(i, int) and i == CHUNKS - 1
                w = LASTN if end else CH
                dve.bn_stats(bnE[:, i, :] if isinstance(i, int) else bnE[:, bass.ds(i, 1), :].rearrange("p a n -> p (a n)"),
                             edge_cols[:, bass.ds(i * CH, w)]).then_inc(e_bn, 1)
                if not (isinstance(i, int) and i == 0):
                    unit_c(*prev(i, j, p))
            steps(dve, 0, CHUNKS, edge1, tail=1)

            def norm(g, b, k):
                dve.wait_ge(e_bn, (k + 1) * CHUNKS)
                dve.bn_aggr(mvE[:, 0:2], bnE[:, :, :].rearrange("p n s -> p (n s)")).then_inc(m_aff, 1)
                dve.wait_ge(m_st, k + 1)
                link(dve.reciprocal(mvE[:, 5:6], mvE[:, 2:3]))
                dve.tensor_tensor(mvE[:, 3:4], mvE[:, 5:6], par[:, g:g + 1], ALU.mult).then_inc(m_aff, 1)
                dve.wait_ge(m_aff, 3 * k + 2)
                link(dve.tensor_tensor(mvE[:, 6:7], mvE[:, 0:1], mvE[:, 3:4], ALU.mult))
                dve.tensor_tensor(mvE[:, 4:5], par[:, b:b + 1], mvE[:, 6:7], ALU.subtract).then_inc(m_aff, 1)

            norm(0, 1, 0)

            def edge2(i, j, p):
                dve.wait_ge(f_mm, i + 1)
                end = isinstance(i, int) and i == CHUNKS - 1
                dve.bn_stats(bnE[:, i, :] if isinstance(i, int) else bnE[:, bass.ds(i, 1), :].rearrange("p a n -> p (a n)"),
                             PE_[p][:, 0:LASTN if end else CH]).then_inc(e_bn, 1)
                dve.tensor_copy(edge_cols[:, cols(i)], PE_[p][:, :]).then_inc(f_c, 1)
            steps(dve, 0, CHUNKS, edge2, tail=1)
            dve.wait_ge(f_c, CHUNKS)
            norm(2, 3, 1)

            def mean0(i, j, p):
                dve.wait_ge(k_T, i + 1)
                ge(dve, k_st[p], 16 * j)
                dve.tensor_tensor(tiles(tr[:, p, :], T), tiles(PE_[p][:, :], T),
                                  spread(inv_cnt[:, bass.ds(i * T, T)], T), ALU.mult).then_inc(k_m, 1)

            dve.wait_ge(s_sameb, 32)

            def edge3(i, j, p):
                dve.wait_ge(k_r, i + 1)
                ge(dve, k_T, i - 1)
                ge(dve, k_sc, i)
                first = isinstance(i, int) and i == 0
                dve.tensor_tensor_scan(sc[:, p, :], same[:, cols(i)], rl[:, p, :],
                                       0.0 if first else sc[:, 1 - p, CH - 1:CH], ALU.mult, ALU.add).then_inc(k_sc, 1)
                if not first:
                    mean0(*prev(i, j, p))
            steps(dve, 0, CHUNKS, edge3)
            end = (CHUNKS - 1, (CHUNKS - 1) // 2, (CHUNKS - 1) % 2)
            mean0(*end)

            def dense(u, j, p):
                unit_a(u, j, p)
                unit_b(u, j, p)
                unit_c(*prev(u, j, p))
            steps(dve, CHUNKS, UNITS, dense)
            unit_c(UNITS - 1, (UNITS - 1) // 2, (UNITS - 1) % 2)

            def sum1(i, j, p):
                dve.wait_ge(l_ev, 2 * i + 1)
                ge(dve, l_t, i - 1)
                ge(dve, l_sc, i)
                first = isinstance(i, int) and i == 0
                dve.tensor_tensor_scan(sc[:, p, :], same[:, cols(i)], edge_cols[:, cols(i)],
                                       0.0 if first else sc[:, 1 - p, CH - 1:CH], ALU.mult, ALU.add).then_inc(l_sc, 1)

            def t1(i, j, p):
                dve.wait_ge(l_t, i + 1)
                ge(dve, l_tst[p], 16 * j)
                ge(dve, l_h, i - 1)
                dve.tensor_tensor(tiles(tr[:, p, :], T), tiles(PE_[0][:, :], T),
                                  spread(inv_cnt[:, bass.ds(i * T, T)], T), ALU.mult).then_inc(l_tu, 1)

            def edge5(i, j, p):
                first = isinstance(i, int) and i == 0
                dve.wait_ge(l_ld[p], 48 * (j + 1))
                dve.wait_ge(l_g[p], 64 * (j + 1))
                ge(dve, l_T, 2 * i)
                ge(dve, l_y, i)
                dve.tensor_tensor(hT[:, :], xb[:, p, :], ob[:, p, :], ALU.add).then_inc(l_z, 1)
                dve.wait_ge(l_z, i + 1)
                dve.scalar_tensor_tensor(sq[:, :], hT[:, :], 0.0, xb[:, p, :], ALU.max, ALU.add).then_inc(l_x, 1)
                dve.wait_ge(l_x, i + 1)
                moments(sq[:, :], G, l_bn, l_q, l_var, i)
                if not first:
                    sum1(*prev(i, j, p))
                dve.wait_ge(l_std, i + 1)
                dve.reciprocal(small[:, 7, :], small[:, 3, :]).then_inc(l_r, 1)
                dve.wait_ge(l_r, i + 1)
                dve.tensor_tensor(tiles(yb[:, :], G), tiles(sq[:, :], G), spread(small[:, 7, :], G), ALU.mult).then_inc(l_y, 1)
                if not first:
                    t1(*prev(i, j, p))
            steps(dve, 0, CHUNKS, edge5)
            sum1(*end)
            t1(*end)
            dve.wait_ge(l_bst[0], 16 * ((CHUNKS + 1) // 2))
            dve.wait_ge(l_bst[1], 16 * (CHUNKS // 2))
            dve.wait_ge(l_tst[0], 16 * ((CHUNKS + 1) // 2))
            dve.wait_ge(l_tst[1], 16 * (CHUNKS // 2))

            def sum_squares(i, j, p):
                dve.wait_ge(o_sq, i + 1)
                dve.tensor_reduce(small[:, 5, 0:T], tiles(half(sq, p), T), AX.X, ALU.add).then_inc(o_red, 1)

            def normalise(i, j, p):
                dve.wait_ge(o_std, i + 1)
                dve.reciprocal(small[:, 7, 0:T], small[:, 6, 0:T]).then_inc(o_rs, 1)
                ge(dve, o_st[p], 64 * j)
                dve.wait_ge(o_rs, i + 1)
                dve.tensor_tensor(tiles(ob[:, p, 0:CH], T), tiles(tr[:, p, :], T), spread(small[:, 7, 0:T], T), ALU.mult).then_inc(o_out, 1)

            def edge6(i, j, p):
                first = isinstance(i, int) and i == 0
                dve.wait_ge(o_r, i + 1)
                ge(dve, o_a, i - 1)
                ge(dve, o_sc, i)
                dve.tensor_tensor_scan(sc[:, p, :], same[:, cols(i)], rl[:, p, :],
                                       0.0 if first else sc[:, 1 - p, CH - 1:CH], ALU.mult, ALU.add).then_inc(o_sc, 1)
                if not first:
                    sum_squares(*prev(i, j, p))
                dve.wait_ge(o_a, i + 1)
                dve.tensor_tensor(tiles(dx[:, :], T), tiles(PE_[1][:, :], T),
                                  spread(inv_cnt[:, bass.ds(i * T, T)], T), ALU.mult).then_inc(o_m, 1)
                dve.wait_ge(o_b[p], 16 * (j + 1))
                dve.wait_ge(o_m, i + 1)
                dve.tensor_tensor(tr[:, p, :], dx[:, :], xb[:, p, 0:CH], ALU.add).then_inc(o_z, 1)
                if not first:
                    normalise(*prev(i, j, p))
            steps(dve, 0, CHUNKS, edge6)
            sum_squares(*end)
            normalise(*end)


_NAMES = ['x', 'src', 'dst', 'L0_gnn_theta_w', 'L0_gnn_phi_w', 'L0_gnn_fc1_w', 'L0_gnn_bn0_g', 'L0_gnn_bn0_b',
          'L0_gnn_bn1_g', 'L0_gnn_bn1_b', 'L1_gnn_W1l', 'L1_gnn_b1l', 'L1_gnn_W1r', 'L1_gnn_W2l', 'L1_gnn_b2l',
          'L1_gnn_W2r']


def kernel(**inputs):
    import numpy as _np
    import concourse.bacc as _bacc
    from concourse import mybir as _mybir
    from concourse.bass_utils import run_bass_kernel_spmd as _run

    nc = _bacc.Bacc("TRN2", target_bir_lowering=False, num_devices=1)
    arrays, args = {}, []
    for name in _NAMES:
        a = _np.ascontiguousarray(inputs[name])
        arrays[f"in_{name}"] = a
        args.append(nc.dram_tensor(f"in_{name}", a.shape, _mybir.dt.from_np(a.dtype), kind="ExternalInput").ap())
    shape = inputs['x'].shape
    args.append(nc.dram_tensor("out_rows", shape, _mybir.dt.float32, kind="ExternalOutput").ap())
    gnn_program(nc, *args)
    r = _run(nc, [arrays], core_ids=[0])
    return r.results[0]["out_rows"]
```

```python
import concourse.bass as bass
from concourse import mybir
from contextlib import ExitStack



def gnn_program(nc, x, src, dst, theta_w, phi_w, fc1_w, bn0_g, bn0_b, bn1_g, bn1_b,
                w1l, b1, w1r, w2l, b2, w2r, out):
    f32, i32, bf16, u8 = mybir.dt.float32, mybir.dt.int32, mybir.dt.bfloat16, mybir.dt.uint8
    ALU, ACT, AX = mybir.AluOpType, mybir.ActivationFunctionType, mybir.AxisListType
    P = 128
    N, C = x.shape
    E = src.shape[0]
    EPS = 1e-5
    T = 4
    CH = T * P
    CHUNKS = -(-E // CH)
    EP = CHUNKS * CH
    TILES = EP // P
    LASTN = E - (CHUNKS - 1) * CH
    B = 2
    Q = TILES // B
    G = 8
    UN = G * P
    UNITS = -(-N // UN)
    HALF = UN // 2
    Z = P
    PZ = 80
    assert E % P and CHUNKS % 2 == 1 and TILES == B * Q and Q <= P and N % PZ == 0 and UNITS == 2 * CHUNKS

    def scratch(name, shape, dt):
        return nc.dram_tensor(name, shape, dt, kind="Internal").ap()

    dst_pad = scratch("dst_pad", [EP + 2], i32)
    src_pad = scratch("src_pad", [EP], i32)
    same_row = scratch("same_row", [EP], u8)
    position = scratch("position", [N, 1], i32)
    xs_spill = scratch("xs_spill", [CHUNKS, P, CH], f32)
    xd_spill = scratch("xd_spill", [CHUNKS, P, CH], f32)
    mean0_tab = scratch("mean0_tab", [Z + EP, C], f32)
    t1_tab = scratch("t1_tab", [Z + EP, C], f32)
    base2 = scratch("base2", [CHUNKS, P, CH], f32)

    ctx = ExitStack()
    with ctx:
        def sb(name, shape, dt=f32):
            return ctx.enter_context(nc.sbuf_tensor(name, shape, dt))

        def pb(name, shape):
            return ctx.enter_context(nc.psum_tensor(name, shape, f32))

        def sem(name):
            return ctx.enter_context(nc.semaphore(name))

        def sems(name):
            return [sem(f"{name}{k}") for k in range(2)]

        edge_cols = sb("edge_cols", [P, EP])
        same = sb("same", [P, EP], u8)
        ident = sb("ident", [P, P])
        centre = sb("centre", [P, P])
        w_in = sb("w_in", [P, 7, P])
        thT, phT, fcT = (sb(n, [P, P]) for n in ("thT", "phT", "fcT"))
        w1lT, w1rT, w2lT, w2rT = (sb(n, [P, P]) for n in ("w1lT", "w1rT", "w2lT", "w2rT"))
        w_mean = sb("w_mean", [P, 8])
        par = sb("par", [P, 8])
        eps = sb("eps", [P, 1])
        b2_all = sb("b2_all", [P, P])
        b2_part = sb("b2_part", [P, 3, P])
        b2_bf = sb("b2_bf", [P, P], bf16)
        b2_rows = sb("b2_rows", [P, CH], bf16)
        ones_bf = sb("ones_bf", [P, P], bf16)
        ones1 = sb("ones1", [1, 1])
        inv_cnt = sb("inv_cnt", [P, TILES])
        gather1 = sb("gather1", [P, CHUNKS, 2 * T], i32)
        scat_idx = sb("scat_idx", [P, TILES], i32)
        row_of = sb("row_of", [P, TILES], i32)
        pos_idx = sb("pos_idx", [P, TILES], i32)
        lane = sb("lane", [P, T], i32)
        idx_stage = sb("idx_stage", [P, 2, 2 * T], i32)
        val_stage = sb("val_stage", [P, 2, T], i32)
        got_stage = sb("got_stage", [P, 2, T], i32)
        max_stage = sb("max_stage", [P, 2, T], i32)
        xb = sb("xb", [P, 2, UN])
        yb = sb("yb", [P, UN])
        yT = sb("yT", [P, UN])
        hT = sb("hT", [P, UN])
        sq = sb("sq", [P, UN])
        ob = sb("ob", [P, 2, UN])
        bn = sb("bn", [P, G, 6])
        small = sb("small", [P, 8, G])
        g1 = sb("g1", [P, 2, 2 * CH])
        dx = sb("dx", [P, CH])
        dT = sb("dT", [P, 2, CH])
        bnE = sb("bnE", [P, CHUNKS, 6])
        mvE = sb("mvE", [P, 8])
        rl = sb("rl", [P, 2, CH])
        sc = sb("sc", [P, 2, CH])
        tr = sb("tr", [P, 2, CH])

        PA = pb("PA", [P, UN])
        PC = pb("PC", [P, UN])
        PD = pb("PD", [P, UN])
        PE_ = [PD[:, 0:CH], PD[:, CH:2 * CH], pb("PE2", [P, CH]), pb("PE3", [P, CH])]

        def ge(e, s, v):
            if not (isinstance(v, int) and v <= 0):
                e.wait_ge(s, v)

        def wait_apart(e, s, v):
            e.wait_ge(s, v)
            e.sem_inc(s_apart, 1)

        def steps(e, first, last, body, head=2, tail=0):
            i = first
            while i < last and (i < first + head or i % 2):
                body(i, i // 2, i % 2)
                i += 1
            stop = max(i // 2, (last - tail) // 2)
            if stop > i // 2:
                with e.Fori(i // 2, stop) as j:
                    body(j * 2, j, 0)
                    body(j * 2 + 1, j, 1)
            for i in range(2 * stop if stop > i // 2 else i, last):
                body(i, i // 2, i % 2)

        def prev(i, j, p):
            return (i - 1, (i - 1) // 2, 1 - p) if isinstance(i, int) else (i - 1, j - 1 + p, 1 - p)

        def following(i, j, p):
            return (i + 1, (i + 1) // 2, 1 - p) if isinstance(i, int) else (i + 1, j + p, 1 - p)

        final = (CHUNKS - 1, (CHUNKS - 1) // 2, (CHUNKS - 1) % 2)
        final_unit = (UNITS - 1, (UNITS - 1) // 2, (UNITS - 1) % 2)

        def half(t, h):
            return t[:, h * HALF:(h + 1) * HALF]

        def tiles(ap, n):
            return ap.rearrange("p (t c) -> p t c", t=n)

        def cols(i):
            return bass.ds(i * CH, CH)

        s_apart = sem("waited")
        s_par, s_tlay, s_w = sem("params_loaded"), sem("targets_loaded"), sem("weights_loaded")
        s_pad, s_pads = sem("pad_tiles_set"), sem("padded_rows_written")
        s_zero, s_same, s_sameb = sem("tables_zeroed"), sem("same_row_written"), sem("same_loaded")
        s_id, s_cst = sem("identity_built"), sem("constants_set")
        s_row, s_dv, s_rowT, s_carry, s_carryT = (sem(n) for n in (
            "row_ready", "dve_setup", "row_transposed", "carry_ready", "carry_transposed"))
        s_lay, s_layT, s_idx = sem("layout_ready"), sem("layout_transposed"), sem("indices_ready")
        s_wc, s_wT, s_wR, s_b2 = (sem(n) for n in ("weights_centred", "weights_transposed", "weights_ready", "b2_ready"))
        b_x, b_st = sems("unit_loaded"), sems("unit_stored")
        b_z, b_bn, b_q = sem("z_ready"), sem("unit_stats"), sem("unit_stats_sum")
        b_var, b_std, b_r, b_y = (sem(n) for n in ("var_ready", "std_ready", "rstd_ready", "y_ready"))
        b_T, b_yT, b_w1, b_h, b_w2 = (sem(n) for n in ("y_transposed", "yT_ready", "w1_done", "h_ready", "w2_done"))
        b_sq, b_red, b_std2, b_r2, b_out = (sem(n) for n in ("squares_ready", "squares_summed", "std2_ready", "rstd2_ready", "unit_out"))
        p_idx = sem("indices_staged")
        e_g, e_sp = sems("x_rows_gathered"), sems("x_rows_spilled")
        e_dd, e_T, e_ev, e_mm, e_c, e_bn = (sem(n) for n in (
            "difference_ready", "rows_transposed", "columns_ready", "edge_product", "edge_copied", "edge_stats"))
        m_st, m_aff = sem("norm_std"), sem("norm_affine")
        f_r, f_mm, f_c = sem("relu0_ready"), sem("fc1_done"), sem("fc1_copied")
        q_set, q_get = sems("positions_set"), sems("positions_got")
        q_max = sem("positions_masked")
        k_r, k_sc, k_T, k_m = sem("relu1_ready"), sem("sum0_ready"), sem("sum0_transposed"), sem("mean0_ready")
        k_st = sems("mean0_stored")
        l_ld, l_g = sems("chunk_loaded"), sems("mean0_gathered")
        l_x, l_z, l_bn, l_q, l_var, l_std, l_r, l_y = (sem("l_" + n) for n in (
            "x1_ready", "z_ready", "stats", "stats_sum", "var_ready", "std_ready", "rstd_ready", "y_ready"))
        l_T, l_ev, l_sc, l_t, l_tu, l_h, l_hr, l_w2, l_b = (sem("l_" + n) for n in (
            "y_transposed", "y_columns", "sum1_ready", "sum1_projected", "t1_ready", "h_product", "h_ready", "w2_done", "base2_ready"))
        l_y2 = sem("l_target_y_ready")
        l_tst, l_bst = sems("t1_stored"), sems("base2_stored")
        o_g, o_b, o_st = sems("t1_gathered"), sems("base2_loaded"), sems("rows_scattered")
        o_h, o_r, o_sc, o_a, o_m, o_z, o_sq, o_red, o_std, o_rs, o_out = (sem("o_" + n) for n in (
            "h_product", "h_ready", "sum2_ready", "sum2_projected", "mean2_ready", "z_ready", "squares_ready",
            "squares_summed", "std_ready", "rstd_ready", "out_ready"))

        RL = 7
        rl_i = sq[:, :]
        def lay_i(k):
            return tiles(ob[:, k // 2, (k % 2) * HALF:(k % 2) * HALF + B * P].bitcast(i32), B)[0:Q]
        def lay(k):
            t = (xb[:, 0], xb[:, 1], yb, yT, hT)[k // 4] if k >= 8 else xb[:, k // 4]
            return tiles(t[:, (k % 4) * B * P:(k % 4) * B * P + B * P], B)[0:Q]
        START, S_, EIDX, SCAN, CNT, INV, ENDF, DM, DSC, XDI, SRCF, ONE = range(12)
        SAME8 = tiles(dT[:, 0, 0:B * P // 4].bitcast(u8), B)[0:Q]
        carry = sc[0:1, 0, 0:TILES + 1]
        row_ps = PE_[0][0:1, 0:TILES]
        carry_ps = PE_[1][0:Q, 0:B]
        lay_ps = PA

        block = ctx.enter_context(nc.Block())

        def unit_rows(t, u):
            at = N - UN if isinstance(u, int) and u == UNITS - 1 else u * UN
            return t[bass.ds(at, UN), :].rearrange("(p g) c -> p (g c)", p=P)

        def chunk_rows(tab, i):
            return tab[bass.ds(i * CH + Z, CH), :].rearrange("(t p) c -> p t c", p=P)

        @block.sync
        def _(sp):
            for k, w in enumerate((theta_w, phi_w, fc1_w, w1l, w1r, w2l, w2r)):
                sp.dma_start(w_in[:, k, :], w).then_inc(s_w, 16)
            sp.wait_ge(s_pad, 1)
            sp.dma_start(dst_pad[bass.ds(1, E)], dst).then_inc(s_pads, 16)
            sp.dma_start(src_pad[bass.ds(0, E)], src).then_inc(s_pads, 16)
            sp.dma_start(dst_pad[bass.ds(0, 1)].rearrange("(a n) -> a n", a=1), idx_stage[0:1, 0, 0:1]).then_inc(s_pads, 16)
            sp.dma_start(dst_pad[bass.ds(1 + E, EP + 1 - E)].rearrange("(a n) -> a n", a=1),
                         pos_idx[0:1, 0:EP + 1 - E]).then_inc(s_pads, 16)
            sp.dma_start(src_pad[bass.ds(E, EP - E)].rearrange("(a n) -> a n", a=1),
                         row_of[0:1, 0:EP - E]).then_inc(s_pads, 16)
            sp.wait_ge(s_pads, 80)
            for k in range(3):
                sp.dma_start(lay_i(k), dst_pad[bass.ds(k, EP)].rearrange("(b q n) -> q b n", b=B, q=Q)).then_inc(s_tlay, 16)
            sp.dma_start(lay_i(3), src_pad.rearrange("(b q n) -> q b n", b=B, q=Q)).then_inc(s_tlay, 16)
            for k, v in enumerate((bn0_g, bn0_b, bn1_g, bn1_b, b1)):
                sp.dma_start(par[:, k:k + 1], v.rearrange("(p a) -> p a", a=1)).then_inc(s_par, 16)
            sp.dma_start(b2_all[:, :], b2.rearrange("(a n) -> a n", a=1).to_broadcast([P, C])).then_inc(s_par, 16)
            sp.wait_ge(s_same, 1)
            sp.dma_start(same_row.rearrange("(b q n) -> q b n", b=B, q=Q), SAME8).then_inc(s_sameb, 16)
            sp.wait_ge(s_sameb, 16)
            sp.dma_start(same[:, :], same_row.rearrange("(a n) -> a n", a=1).to_broadcast([P, EP])).then_inc(s_sameb, 16)
            sp.dma_start(position.rearrange("(p n) a -> p (n a)", p=PZ),
                         edge_cols[0:PZ, 0:N // PZ].bitcast(i32)).then_inc(s_zero, 16)
            sp.dma_start(mean0_tab[0:Z, :], edge_cols[:, 0:C]).then_inc(s_zero, 16)
            sp.dma_start(t1_tab[0:Z, :], edge_cols[:, 0:C]).then_inc(s_zero, 16)
            sp.wait_ge(s_idx, 1)
            def load_unit(u, j, p):
                ge(sp, b_y, u - 1)
                sp.dma_start(xb[:, p, :], unit_rows(x, u)).then_inc(b_x[p], 16)

            def store_unit(u, j, p):
                ge(sp, b_out, u + 1)
                if isinstance(u, int) and u == UNITS - 1:
                    sp.wait_ge(b_st[1 - p], 16 * (j + 1))
                sp.dma_start(unit_rows(out, u), ob[:, p, :]).then_inc(b_st[p], 16)

            load_unit(0, 0, 0)

            def edge1(i, j, p):
                load_unit(*following(i, j, p))
                sp.wait_ge(e_g[p], 128 * (j + 1))
                sp.dma_start(xs_spill[i] if isinstance(i, int) else xs_spill[bass.ds(i, 1)].rearrange("a p n -> (a p) n"),
                             g1[:, p, 0:CH]).then_inc(e_sp[p], 16)
                sp.dma_start(xd_spill[i] if isinstance(i, int) else xd_spill[bass.ds(i, 1)].rearrange("a p n -> (a p) n"),
                             g1[:, p, CH:2 * CH]).then_inc(e_sp[p], 16)
                if not (isinstance(i, int) and i < 2):
                    store_unit(i - 2, j - 1, p)
            steps(sp, 0, CHUNKS, edge1)

            def store_mean0(i, j, p):
                sp.wait_ge(k_m, i + 1)
                sp.dma_start(chunk_rows(mean0_tab, i), tiles(tr[:, p, :], T)).then_inc(k_st[p], 16)
            steps(sp, 0, CHUNKS, store_mean0)

            def dense(u, j, p):
                if not (isinstance(u, int) and u == UNITS - 1):
                    load_unit(*following(u, j, p))
                store_unit(u - 2, j - 1, p)
            steps(sp, CHUNKS, UNITS, dense, tail=2)
            store_unit(*prev(*final_unit))
            store_unit(*final_unit)
            sp.wait_ge(k_st[0], 16 * ((CHUNKS + 1) // 2))
            sp.wait_ge(k_st[1], 16 * (CHUNKS // 2))
            sp.wait_ge(e_sp[0], 32 * ((CHUNKS + 1) // 2))
            sp.wait_ge(e_sp[1], 32 * (CHUNKS // 2))
            sp.wait_ge(b_y, UNITS)

            def at(t, i):
                return t[i] if isinstance(i, int) else t[bass.ds(i, 1)].rearrange("a p n -> (a p) n")

            def load5(i, j, p):
                ge(sp, l_x, i - 1)
                sp.dma_start(xb[:, p, 0:CH], at(xs_spill, i)).then_inc(l_ld[p], 16)
                sp.dma_start(xb[:, p, CH:2 * CH], at(xd_spill, i)).then_inc(l_ld[p], 16)
                sp.dma_start(tiles(ob[:, p, CH:2 * CH], T), chunk_rows(mean0_tab, i)).then_inc(l_ld[p], 16)

            def store_t1(i, j, p):
                sp.wait_ge(l_tu, i + 1)
                sp.dma_start(chunk_rows(t1_tab, i), tiles(tr[:, p, :], T)).then_inc(l_tst[p], 16)

            def store_base(i, j, p):
                sp.wait_ge(l_b, i + 1)
                sp.dma_start(at(base2, i), rl[:, p, :]).then_inc(l_bst[p], 16)

            load5(0, 0, 0)

            def edge5(i, j, p):
                if not (isinstance(i, int) and i == CHUNKS - 1):
                    load5(*following(i, j, p))
                if not (isinstance(i, int) and i < 1):
                    store_t1(*prev(i, j, p))
                if not (isinstance(i, int) and i < 2):
                    store_base(i - 2, j - 1, p)
            steps(sp, 0, CHUNKS, edge5, tail=1)
            store_t1(*final)
            store_base(*prev(*final))
            store_base(*final)
            sp.wait_ge(l_bst[0], 16 * ((CHUNKS + 1) // 2))
            sp.wait_ge(l_bst[1], 16 * (CHUNKS // 2))
            sp.wait_ge(l_y, CHUNKS)

            def load6(i, j, p):
                ge(sp, o_z, i - 1)
                sp.dma_start(xb[:, p, 0:CH], at(base2, i)).then_inc(o_b[p], 16)
            steps(sp, 0, CHUNKS, load6)

        @block.gpsimd
        def _(gp):
            gp.memset(ident[:, :], 0.0).then_inc(s_id, 1)
            gp.wait_ge(s_id, 1)
            gp.affine_select(out=ident[:, :], in_=ident[:, :], compare_op=ALU.not_equal, fill=1.0,
                             base=0, pattern=[[-1, P]], channel_multiplier=1).then_inc(s_id, 1)
            gp.iota(lay(EIDX), [[Q * P, B], [1, P]], base=0, channel_multiplier=P,
                    allow_small_or_imprecise_dtypes=True).then_inc(s_id, 1)
            gp.iota(lane[:, :], [[0, T]], base=0, channel_multiplier=1).then_inc(s_id, 1)
            gp.wait_ge(s_pads, 80)
            gp.iota(row_of[:, :], [[P, TILES]], base=Z, channel_multiplier=1).then_inc(s_id, 1)
            gp.wait_ge(s_id, 5)
            gp.wait_ge(s_idx, 1)

            def rows(i, j, p):
                ge(gp, e_sp[p], 32 * j)
                ge(gp, e_dd, i - 1)
                ge(gp, e_T, i - 1)
                gp.tensor_copy(idx_stage[:, p, :], gather1[:, i, :] if isinstance(i, int)
                               else gather1[:, bass.ds(i, 1), :].rearrange("p a n -> p (a n)")).then_inc(p_idx, 1)
                wait_apart(gp, p_idx, i + 1)
                for t in range(2 * T):
                    gp.indirect_dma_start(g1[:, p, t * C:(t + 1) * C], None, x,
                                          bass.IndirectOffsetOnAxis(ap=idx_stage[:, p, t:t + 1], axis=0)).then_inc(e_g[p], 16)
            steps(gp, 0, CHUNKS, rows)

            gp.wait_ge(s_zero, 48)
            P1 = CHUNKS
            def set_pos(i, j, p):
                ge(gp, q_set[p], 64 * j)
                gp.tensor_copy(idx_stage[:, p, 0:T], scat_idx[:, bass.ds(i * T, T)]).then_inc(p_idx, 1)
                gp.tensor_copy(val_stage[:, p, :], row_of[:, bass.ds(i * T, T)]).then_inc(p_idx, 1)
                wait_apart(gp, p_idx, P1 + 2 * i + 2)
                for t in range(T):
                    gp.indirect_dma_start(position, bass.IndirectOffsetOnAxis(ap=idx_stage[:, p, t:t + 1], axis=0),
                                          val_stage[:, p, t:t + 1], None, bounds_check=N - 1, oob_is_err=False).then_inc(q_set[p], 16)
            gp.wait_ge(e_g[0], 128 * ((CHUNKS + 1) // 2))
            gp.wait_ge(e_g[1], 128 * (CHUNKS // 2))
            steps(gp, 0, CHUNKS, set_pos)
            gp.wait_ge(q_set[0], 64 * ((CHUNKS + 1) // 2))
            gp.wait_ge(q_set[1], 64 * (CHUNKS // 2))

            P2 = 3 * CHUNKS
            def mask_pos(i, j, p):
                wait_apart(gp, q_get[p], 64 * (j + 1))
                gp.tensor_scalar(max_stage[:, p, :], got_stage[:, p, :], lane[:, 0:1], None, ALU.max).then_inc(q_max, 1)
                wait_apart(gp, q_max, 2 * i + 1)
                gp.tensor_copy(pos_idx[:, bass.ds(i * T, T)], max_stage[:, p, :]).then_inc(q_max, 1)

            def get_pos(i, j, p):
                ge(gp, q_max, 2 * i - 2)
                gp.tensor_copy(idx_stage[:, p, 0:T], gather1[:, i, 0:T] if isinstance(i, int)
                               else gather1[:, bass.ds(i, 1), 0:T].rearrange("p a n -> p (a n)")).then_inc(p_idx, 1)
                wait_apart(gp, p_idx, P2 + i + 1)
                for t in range(T):
                    gp.indirect_dma_start(got_stage[:, p, t:t + 1], None, position,
                                          bass.IndirectOffsetOnAxis(ap=idx_stage[:, p, t:t + 1], axis=0)).then_inc(q_get[p], 16)
                if not (isinstance(i, int) and i == 0):
                    mask_pos(*prev(i, j, p))
            steps(gp, 0, CHUNKS, get_pos)
            mask_pos(CHUNKS - 1, (CHUNKS - 1) // 2, (CHUNKS - 1) % 2)
            wait_apart(gp, q_max, 2 * CHUNKS)

            gp.wait_ge(k_st[0], 16 * ((CHUNKS + 1) // 2))
            gp.wait_ge(k_st[1], 16 * (CHUNKS // 2))
            gp.wait_ge(b_st[0], 16 * (UNITS // 2))
            gp.wait_ge(b_st[1], 16 * (UNITS // 2))
            P3 = 4 * CHUNKS
            def gather5(i, j, p):
                ge(gp, l_x, i - 1)
                gp.tensor_copy(idx_stage[:, p, 0:T], pos_idx[:, bass.ds(i * T, T)]).then_inc(p_idx, 1)
                wait_apart(gp, p_idx, P3 + i + 1)
                for t in range(T):
                    gp.indirect_dma_start(ob[:, p, t * C:(t + 1) * C], None, mean0_tab,
                                          bass.IndirectOffsetOnAxis(ap=idx_stage[:, p, t:t + 1], axis=0)).then_inc(l_g[p], 16)
            steps(gp, 0, CHUNKS, gather5)

            gp.wait_ge(l_tst[0], 16 * ((CHUNKS + 1) // 2))
            gp.wait_ge(l_tst[1], 16 * (CHUNKS // 2))
            P4 = 5 * CHUNKS
            def gather6(i, j, p):
                ge(gp, o_h, i - 1)
                gp.tensor_copy(idx_stage[:, p, 0:T], pos_idx[:, bass.ds(i * T, T)]).then_inc(p_idx, 1)
                if isinstance(i, int) and i < 2:
                    wait_apart(gp, p_idx, P4 + i + 1)
                else:
                    wait_apart(gp, p_idx, P4 + 2 * i - 1)
                for t in range(T):
                    gp.indirect_dma_start(g1[:, p, t * C:(t + 1) * C], None, t1_tab,
                                          bass.IndirectOffsetOnAxis(ap=idx_stage[:, p, t:t + 1], axis=0)).then_inc(o_g[p], 16)

            def scatter6(i, j, p):
                ge(gp, o_st[p], 64 * j)
                gp.wait_ge(o_out, i + 1)
                gp.tensor_copy(idx_stage[:, p, T:2 * T], scat_idx[:, bass.ds(i * T, T)]).then_inc(p_idx, 1)
                wait_apart(gp, p_idx, P4 + 2 * CHUNKS - 1 + i - (CHUNKS - 2) if isinstance(i, int) and i >= CHUNKS - 2 else P4 + 2 * i + 4)
                for t in range(T):
                    gp.indirect_dma_start(out, bass.IndirectOffsetOnAxis(ap=idx_stage[:, p, T + t:T + t + 1], axis=0),
                                          ob[:, p, t * C:(t + 1) * C], None, bounds_check=N - 1, oob_is_err=False).then_inc(o_st[p], 16)
            gather6(0, 0, 0)
            gather6(1, 0, 1)

            def turn6(i, j, p):
                gather6(i, j, p)
                scatter6(i - 2, j - 1, p)
            steps(gp, 2, CHUNKS, turn6, head=0)
            scatter6(CHUNKS - 2, (CHUNKS - 2) // 2, (CHUNKS - 2) % 2)
            scatter6(CHUNKS - 1, (CHUNKS - 1) // 2, (CHUNKS - 1) % 2)
            gp.wait_ge(o_st[0], 64 * ((CHUNKS + 1) // 2))
            gp.wait_ge(o_st[1], 64 * (CHUNKS // 2))
            gp.wait_ge(s_zero, 48)

        @block.scalar
        def _(act):
            def root(o, i, s, e):
                return act.activation(o, i, ACT.Sqrt, bias=eps[:, 0:1], scale=s)

            def unit_root1(u, j, p):
                act.wait_ge(b_var, u + 1)
                root(small[:, 3, :], small[:, 2, :], 1.0 / C, EPS).then_inc(b_std, 1)

            def unit_columns(u, j, p):
                for h in range(2):
                    act.wait_ge(b_T, 2 * u + 1 + h)
                    ge(act, b_w2, 2 * u - 1 + h)
                    act.activation(half(yT, h), half(PA, h), ACT.Copy).then_inc(b_yT, 1)

            def unit_hidden(u, j, p):
                for h in range(2):
                    act.wait_ge(b_w1, 2 * u + 1 + h)
                    act.activation(half(hT, h), half(PA, h), ACT.Relu, bias=par[:, 4:5]).then_inc(b_h, 1)

            def unit_sum_squares(u, j, p):
                ge(act, b_std2, u)
                for h in range(2):
                    act.wait_ge(b_w2, 2 * u + 1 + h)
                    for t in range(4 * h, 4 * h + 4):
                        last = act.activation(sq[:, t * P:(t + 1) * P], (PC, PD)[p][:, t * P:(t + 1) * P], ACT.Square,
                                              accum_out=small[:, 5, t:t + 1])
                last.then_inc(b_red, 1)

            def unit_squares(u, j, p):
                ge(act, b_red, u)
                for h in range(2):
                    act.wait_ge(b_w2, 2 * u + 1 + h)
                    act.activation(half(sq, h), half(PC, h), ACT.Square).then_inc(b_sq, 1)

            def unit_root2(u, j, p):
                act.wait_ge(b_red, u + 1)
                ge(act, b_r2, u)
                root(small[:, 6, :], small[:, 5, :], 1.0 / C, EPS).then_inc(b_std2, 1)

            act.wait_ge(s_cst, 1)
            act.wait_ge(s_wT, 1)
            act.wait_ge(s_wR, 2)
            act.activation(thT[:, :], PE_[2][:, 0:P], ACT.Copy).then_inc(s_wR, 1)
            act.activation(phT[:, :], PE_[2][:, P:2 * P], ACT.Copy).then_inc(s_wR, 1)
            act.activation(fcT[:, :], PE_[2][:, 2 * P:3 * P], ACT.Copy).then_inc(s_wR, 1)
            act.activation(w1lT[:, :], PE_[2][:, 3 * P:4 * P], ACT.Copy).then_inc(s_wR, 1)
            act.activation(w1rT[:, :], PE_[3][:, 0:P], ACT.Copy).then_inc(s_wR, 1)
            act.wait_ge(s_par, 96)
            act.wait_ge(s_sameb, 32)
            act.wait_ge(s_zero, 48)

            def edge1(i, j, p):
                unit_columns(i, j, p)
                if not (isinstance(i, int) and i == 0):
                    unit_root2(*prev(i, j, p))
                act.wait_ge(e_T, i + 1)
                ge(act, e_mm, i)
                act.activation(dT[:, 0, :], PE_[0][:, :], ACT.Copy).then_inc(e_ev, 1)
                act.activation(dT[:, 1, :], PE_[1][:, :], ACT.Copy).then_inc(e_ev, 1)
                unit_hidden(i, j, p)
                act.wait_ge(e_mm, i + 1)
                act.activation(edge_cols[:, cols(i)], PE_[2][:, :], ACT.Copy).then_inc(e_c, 1)
                if not (isinstance(i, int) and i == CHUNKS - 1):
                    unit_root1(*following(i, j, p))
                unit_squares(i, j, p)
            unit_root1(0, 0, 0)
            steps(act, 0, CHUNKS, edge1, tail=1)

            act.wait_ge(m_aff, 1)
            act.activation(mvE[:, 2:3], mvE[:, 1:2], ACT.Sqrt, bias=eps[:, 0:1]).then_inc(m_st, 1)
            act.wait_ge(m_aff, 3)

            def edge2(i, j, p):
                ge(act, f_mm, i - 1)
                act.activation(rl[:, p, :], edge_cols[:, cols(i)], ACT.Relu, bias=mvE[:, 4:5], scale=mvE[:, 3:4]).then_inc(f_r, 1)
            steps(act, 0, CHUNKS, edge2)
            act.wait_ge(m_aff, 4)
            act.activation(mvE[:, 2:3], mvE[:, 1:2], ACT.Sqrt, bias=eps[:, 0:1]).then_inc(m_st, 1)
            act.wait_ge(m_aff, 6)

            def edge3(i, j, p):
                ge(act, k_sc, i - 1)
                act.activation(rl[:, p, :], edge_cols[:, cols(i)], ACT.Relu, bias=mvE[:, 4:5], scale=mvE[:, 3:4]).then_inc(k_r, 1)
            steps(act, 0, CHUNKS, edge3)

            def dense(u, j, p):
                unit_columns(u, j, p)
                if not (isinstance(u, int) and u == CHUNKS):
                    unit_sum_squares(*prev(u, j, p))
                unit_root2(*prev(u, j, p))
                unit_hidden(u, j, p)
                if not (isinstance(u, int) and u == UNITS - 1):
                    unit_root1(*following(u, j, p))
            unit_root1(CHUNKS, CHUNKS // 2, CHUNKS % 2)
            steps(act, CHUNKS, UNITS, dense, tail=1)
            unit_sum_squares(*final_unit)
            unit_root2(*final_unit)

            def hidden5(i, j, p):
                act.wait_ge(l_h, i + 1)
                ge(act, l_w2, i)
                act.activation(dT[:, 0, :], PE_[1][:, :], ACT.Relu, bias=par[:, 4:5]).then_inc(l_hr, 1)

            def base5(i, j, p):
                act.wait_ge(l_w2, i + 1)
                ge(act, l_bst[p], 16 * j)
                act.activation(rl[:, p, :], PE_[2][:, :], ACT.Copy).then_inc(l_b, 1)

            def edge5(i, j, p):
                act.wait_ge(l_var, i + 1)
                root(small[:, 3, :], small[:, 2, :], 1.0 / C, EPS).then_inc(l_std, 1)
                act.wait_ge(l_r, i + 1)
                ge(act, l_T, 2 * i)
                for t in range(T, 2 * T):
                    last = act.activation(yb[:, t * C:(t + 1) * C], sq[:, t * C:(t + 1) * C], ACT.Copy, scale=small[:, 7, t:t + 1])
                last.then_inc(l_y2, 1)
                act.wait_ge(l_T, 2 * i + 1)
                act.activation(edge_cols[:, cols(i)], half(PA, 0), ACT.Copy).then_inc(l_ev, 1)
                act.wait_ge(l_T, 2 * i + 2)
                ge(act, l_w2, i - 1)
                act.activation(half(yT, p), half(PA, 1), ACT.Copy).then_inc(l_ev, 1)
                if not (isinstance(i, int) and i == 0):
                    hidden5(*prev(i, j, p))
                    base5(*prev(i, j, p))
            steps(act, 0, CHUNKS, edge5)
            hidden5(*final)
            base5(*final)

            def root6(i, j, p):
                act.wait_ge(o_red, i + 1)
                root(small[:, 6, 0:T], small[:, 5, 0:T], 1.0 / C, EPS).then_inc(o_std, 1)

            def edge6(i, j, p):
                if not (isinstance(i, int) and i == 0):
                    root6(*prev(i, j, p))
                act.wait_ge(o_h, i + 1)
                ge(act, o_sc, i - 1)
                act.activation(rl[:, p, :], PE_[0][:, :], ACT.Relu, bias=par[:, 4:5]).then_inc(o_r, 1)
                act.wait_ge(o_z, i + 1)
                act.activation(half(sq, p), tr[:, p, :], ACT.Square).then_inc(o_sq, 1)
            act.wait_ge(l_bst[0], 16 * ((CHUNKS + 1) // 2))
            act.wait_ge(l_bst[1], 16 * (CHUNKS // 2))
            steps(act, 0, CHUNKS, edge6)
            root6(CHUNKS - 1, (CHUNKS - 1) // 2, (CHUNKS - 1) % 2)

        @block.tensor
        def _(pe):
            pe.wait_ge(s_id, 2)
            pe.wait_ge(s_cst, 1)
            pe.wait_ge(s_row, 1)
            for b in range(B):
                last = pe.matmul(row_ps[:, b * Q:(b + 1) * Q], lay(SCAN)[:, b, P - 1:P], ident[0:Q, 0:Q], start=True, stop=True)
            last.then_inc(s_rowT, 1)
            pe.wait_ge(s_carry, 1)
            for b in range(B):
                last = pe.matmul(carry_ps[:, b:b + 1], carry[:, b * Q:(b + 1) * Q], ones1[:, :], start=True, stop=True)
            last.then_inc(s_carryT, 1)
            pe.wait_ge(s_lay, 1)
            for k, row in enumerate((INV, DSC, XDI, SRCF)):
                for b in range(B):
                    at = (k // 2) * HALF + ((k % 2) * B + b) * Q
                    last = pe.transpose(lay_ps[:, at:at + Q], lay(row)[:, b, :], ident[0:Q, 0:Q])
            last.then_inc(s_layT, 1)
            pe.wait_ge(s_wc, 1)
            for k, w in enumerate((0, 1, 2, 3, 4, 5, 6)):
                last = pe.transpose(PE_[2 + k // 4][:, (k % 4) * P:(k % 4 + 1) * P], w_in[:, w, :], ident[:, :])
            last.then_inc(s_wT, 1)
            pe.wait_ge(s_wR, 7)
            pe.wait_ge(s_b2, 1)
            pe.wait_ge(s_idx, 1)

            def unit_transpose(u, j, p):
                pe.wait_ge(b_y, u + 1)
                for h in range(2):
                    ge(pe, b_h, 2 * u - 1 + h)
                    for t in range(4 * h, 4 * h + 4):
                        last = pe.transpose(PA[:, t * P:(t + 1) * P], yb[:, t * P:(t + 1) * P], ident[:, :])
                    last.then_inc(b_T, 1)

            def unit_w1(u, j, p):
                for h in range(2):
                    pe.wait_ge(b_yT, 2 * u + 1 + h)
                    pe.matmul(half(PA, h), w1rT[:, :], half(yT, h), start=True, stop=True).then_inc(b_w1, 1)

            def unit_w2(u, j, p, PC, back):
                ge(pe, b_out, u + 1 - back)
                for h in range(2):
                    pe.matmul(half(PC, h), ones_bf[:, :], b2_rows[:, :], start=True, stop=False)
                    for t in range(4 * h, 4 * h + 4):
                        pe.matmul(PC[:, t * P:(t + 1) * P], yT[:, t * P:(t + 1) * P], centre[:, :], start=False, stop=False)
                for h in range(2):
                    pe.wait_ge(b_h, 2 * u + 1 + h)
                    for t in range(4 * h, 4 * h + 4):
                        last = pe.matmul(PC[:, t * P:(t + 1) * P], hT[:, t * P:(t + 1) * P], w2rT[:, :], start=False, stop=t % 4 == 3)
                    last.then_inc(b_w2, 1)

            def unit(u, j, p):
                unit_transpose(u, j, p)
                unit_w1(u, j, p)
                unit_w2(u, j, p, (PC, PD)[p], 2)

            def edge1(i, j, p):
                unit_transpose(i, j, p)
                pe.wait_ge(e_dd, i + 1)
                for t in range(T):
                    pe.transpose(PE_[0][:, t * P:(t + 1) * P], dx[:, t * C:(t + 1) * C], ident[:, :])
                for t in range(T):
                    last = pe.transpose(PE_[1][:, t * P:(t + 1) * P], g1[:, p, t * C:(t + 1) * C], ident[:, :])
                last.then_inc(e_T, 1)
                unit_w1(i, j, p)
                pe.wait_ge(e_ev, 2 * i + 2)
                ge(pe, e_c, i)
                pe.matmul(PE_[2][:, :], thT[:, :], dT[:, 0, :], start=True, stop=False)
                pe.matmul(PE_[2][:, :], phT[:, :], dT[:, 1, :], start=False, stop=True).then_inc(e_mm, 1)
                unit_w2(i, j, p, PC, 1)
            steps(pe, 0, CHUNKS, edge1)

            def edge2(i, j, p):
                pe.wait_ge(f_r, i + 1)
                ge(pe, f_c, i - 1)
                pe.matmul(PE_[p][:, :], fcT[:, :], rl[:, p, :], start=True, stop=True).then_inc(f_mm, 1)
            steps(pe, 0, CHUNKS, edge2)

            def edge3(i, j, p):
                pe.wait_ge(k_sc, i + 1)
                ge(pe, k_m, i - 1)
                for t in range(T):
                    last = pe.transpose(PE_[p][:, t * P:(t + 1) * P], sc[:, p, t * P:(t + 1) * P], ident[:, :])
                last.then_inc(k_T, 1)
            steps(pe, 0, CHUNKS, edge3)
            pe.wait_ge(k_m, CHUNKS)
            steps(pe, CHUNKS, UNITS, unit)
            pe.wait_ge(b_out, UNITS)

            def head5(i, j, p):
                pe.wait_ge(l_ev, 2 * i + 2)
                ge(pe, l_hr, i)
                pe.matmul(PE_[1][:, :], w1rT[:, :], half(yT, p), start=True, stop=False)
                ge(pe, l_b, i)
                pe.matmul(PE_[2][:, :], ones_bf[:, :], b2_rows[:, :], start=True, stop=False)
                for t in range(T):
                    pe.matmul(PE_[2][:, t * P:(t + 1) * P], yT[:, p * CH + t * P:p * CH + (t + 1) * P], centre[:, :], start=False, stop=False)

            def hidden5(i, j, p):
                pe.wait_ge(l_tu, i + 1)
                for t in range(T):
                    last = pe.matmul(PE_[1][:, t * P:(t + 1) * P], tr[:, p, t * C:(t + 1) * C], ident[:, :], start=False, stop=t == T - 1)
                last.then_inc(l_h, 1)

            def base5(i, j, p):
                pe.wait_ge(l_hr, i + 1)
                for t in range(T):
                    last = pe.matmul(PE_[2][:, t * P:(t + 1) * P], dT[:, 0, t * P:(t + 1) * P], w2rT[:, :], start=False, stop=t == T - 1)
                last.then_inc(l_w2, 1)

            def project5(i, j, p):
                pe.wait_ge(l_sc, i + 1)
                ge(pe, l_tu, i)
                for t in range(T):
                    last = pe.matmul(PE_[0][:, t * C:(t + 1) * C], sc[:, p, t * P:(t + 1) * P], w1lT[:, :], start=True, stop=True)
                last.then_inc(l_t, 1)

            def edge5(i, j, p):
                first = isinstance(i, int) and i == 0
                if not first:
                    project5(*prev(i, j, p))
                    head5(*prev(i, j, p))
                ge(pe, l_ev, 2 * i)
                for h in range(2):
                    pe.wait_ge((l_y, l_y2)[h], i + 1)
                    for t in range(4 * h, 4 * h + 4):
                        last = pe.transpose(PA[:, t * P:(t + 1) * P], yb[:, t * P:(t + 1) * P], ident[:, :])
                    last.then_inc(l_T, 1)
                if not first:
                    hidden5(*prev(i, j, p))
                    base5(*prev(i, j, p))
            steps(pe, 0, CHUNKS, edge5)
            project5(*final)
            head5(*final)
            hidden5(*final)
            base5(*final)

            def edge6(i, j, p):
                pe.wait_ge(o_g[p], 64 * (j + 1))
                ge(pe, o_r, i)
                pe.matmul(PE_[0][:, :], w1rT[:, :], edge_cols[:, cols(i)], start=True, stop=False)
                for t in range(T):
                    last = pe.matmul(PE_[0][:, t * P:(t + 1) * P], g1[:, p, t * C:(t + 1) * C], ident[:, :], start=False, stop=t == T - 1)
                last.then_inc(o_h, 1)
                pe.wait_ge(o_sc, i + 1)
                ge(pe, o_m, i)
                for t in range(T):
                    last = pe.matmul(PE_[1][:, t * C:(t + 1) * C], sc[:, p, t * P:(t + 1) * P], w2lT[:, :], start=True, stop=True)
                last.then_inc(o_a, 1)
            steps(pe, 0, CHUNKS, edge6)

        @block.vector
        def _(dve):
            n = [0]

            def link(ins):
                n[0] += 1
                ins.then_inc(s_dv, 1)
                dve.wait_ge(s_dv, n[0])

            dve.memset(idx_stage[:, :, :], -1)
            dve.memset(row_of[:, :], 0)
            dve.memset(pos_idx[:, :], N).then_inc(s_pad, 1)
            link(dve.memset(edge_cols[:, 0:N // PZ], 0.0))
            dve.memset(lay(ONE), 1.0)
            dve.memset(ones_bf[:, :], 1.0)
            dve.memset(ones1[:, :], 1.0)
            dve.memset(carry[:, 0:1], 0.0)
            dve.memset(eps[:, :], EPS).then_inc(s_cst, 1)
            dve.wait_ge(s_cst, 1)
            dve.wait_ge(s_tlay, 64)
            dve.tensor_tensor(SAME8, lay_i(1), lay_i(0), ALU.is_equal).then_inc(s_same, 1)
            dve.tensor_tensor(lay(START), lay_i(1), lay_i(0), ALU.not_equal)
            dve.tensor_tensor(lay(ENDF), lay_i(1), lay_i(2), ALU.not_equal)
            dve.tensor_scalar(lay(DM), lay_i(1), float(-N), None, ALU.add)
            dve.tensor_scalar(lay(XDI), lay_i(1), float(N - 1), None, ALU.min)
            link(dve.tensor_copy(lay(SRCF), lay_i(3)))
            dve.wait_ge(s_id, 3)
            link(dve.tensor_tensor(lay(S_), lay(START), lay(EIDX), ALU.mult))
            for b in range(B):
                last = dve.tensor_tensor_scan(lay(SCAN)[:, b, :], lay(ONE)[:, b, :], lay(S_)[:, b, :], 0.0, ALU.mult, ALU.max)
            last.then_inc(s_row, 1)
            link(dve.tensor_tensor(lay(DM), lay(DM), lay(ENDF), ALU.mult))
            link(dve.tensor_scalar(lay(DSC), lay(DM), float(N), None, ALU.add))
            dve.wait_ge(s_rowT, 1)
            link(dve.memset(sc[0:1, 1, 0:TILES], 1.0))
            dve.tensor_tensor_scan(carry[:, 1:TILES + 1], sc[0:1, 1, 0:TILES], row_ps, 0.0, ALU.mult, ALU.max).then_inc(s_carry, 1)
            dve.wait_ge(s_carryT, 1)
            for b in range(B):
                last = dve.tensor_scalar(lay(CNT)[:, b, :], lay(SCAN)[:, b, :], carry_ps[:, b:b + 1], -1.0, ALU.max, ALU.add)
            link(last)
            link(dve.tensor_tensor(lay(CNT), lay(EIDX), lay(CNT), ALU.subtract))
            dve.reciprocal(lay(INV), lay(CNT)).then_inc(s_lay, 1)
            dve.wait_ge(s_layT, 1)
            def col(k):
                at = (k // 2) * HALF + (k % 2) * TILES
                return lay_ps[:, at:at + TILES]
            dve.tensor_copy(inv_cnt[:, :], col(0))
            dve.tensor_copy(scat_idx[:, :], col(1))
            dve.tensor_copy(gather1[:, :, T:2 * T], col(2).rearrange("p (n t) -> p n t", t=T))
            dve.tensor_copy(gather1[:, :, 0:T], col(3).rearrange("p (n t) -> p n t", t=T)).then_inc(s_idx, 1)
            dve.wait_ge(s_w, 112)
            dve.wait_ge(s_idx, 1)
            dve.tensor_scalar(centre[:, :], ident[:, :], -1.0 / C, None, ALU.add)
            link(dve.tensor_reduce(w_mean[:, 0:2], w_in[:, 3:5, :], AX.X, ALU.add))
            link(dve.tensor_scalar(w_mean[:, 2:4], w_mean[:, 0:2], -1.0 / C, None, ALU.mult))
            dve.tensor_tensor(w_in[:, 3:5, :], w_in[:, 3:5, :], w_mean[:, 2:4].unsqueeze(2).to_broadcast([P, 2, P]), ALU.add).then_inc(s_wc, 1)
            dve.wait_ge(s_wT, 1)
            w2 = PE_[3][:, P:3 * P].rearrange("p (a c) -> p a c", a=2)
            link(dve.tensor_reduce(w_mean[:, 4:6], w2, AX.X, ALU.add))
            link(dve.tensor_scalar(w_mean[:, 6:8], w_mean[:, 4:6], -1.0 / C, None, ALU.mult))
            dve.tensor_scalar(w2lT[:, :], PE_[3][:, P:2 * P], w_mean[:, 6:7], None, ALU.add)
            dve.tensor_scalar(w2rT[:, :], PE_[3][:, 2 * P:3 * P], w_mean[:, 7:8], None, ALU.add).then_inc(s_wR, 2)
            dve.wait_ge(s_par, 96)
            link(dve.tensor_reduce(w_mean[:, 0:1], b2_all[:, :], AX.X, ALU.add))
            link(dve.tensor_scalar(w_mean[:, 1:2], w_mean[:, 0:1], -1.0 / C, None, ALU.mult))
            link(dve.tensor_scalar(b2_all[:, :], b2_all[:, :], w_mean[:, 1:2], None, ALU.add))
            for k in range(3):
                link(dve.tensor_copy(b2_bf[:, :], b2_all[:, :]))
                link(dve.tensor_copy(b2_part[:, k, :], b2_bf[:, :]))
                link(dve.tensor_tensor(b2_all[:, :], b2_all[:, :], b2_part[:, k, :], ALU.subtract))
            link(dve.tensor_scalar(b2_part[:, 0, :], b2_part[:, 0, :], ident[:, 0:1], None, ALU.mult))
            for k in (1, 2):
                link(dve.scalar_tensor_tensor(b2_part[:, 0, :], b2_part[:, k, :], ident[:, k:k + 1], b2_part[:, 0, :], ALU.mult, ALU.add))
            dve.tensor_copy(b2_rows[:, :].rearrange("p (a c) -> p a c", a=4),
                            b2_part[:, 0:1, :].to_broadcast([P, 4, P])).then_inc(s_b2, 1)

            def spread(v, k):
                return v.unsqueeze(2).to_broadcast([P, k, C])

            def moments(z, k, s_bn, s_q, s_var, i, between=None):
                for t in range(k):
                    last = dve.bn_stats(bn[:, t, :], z[:, t * C:(t + 1) * C])
                last.then_inc(s_bn, 1)
                if between:
                    between()
                dve.wait_ge(s_bn, i + 1)
                dve.tensor_tensor(small[:, 0, 0:k], bn[:, 0:k, 1], bn[:, 0:k, 4], ALU.subtract)
                dve.tensor_tensor(small[:, 1, 0:k], bn[:, 0:k, 2], bn[:, 0:k, 5], ALU.add).then_inc(s_q, 1)
                dve.wait_ge(s_q, 2 * i + 1)
                dve.scalar_tensor_tensor(small[:, 4, 0:k], small[:, 0, 0:k], C / 4.0, small[:, 0, 0:k], ALU.mult, ALU.mult).then_inc(s_q, 1)
                dve.wait_ge(s_q, 2 * i + 2)
                dve.tensor_tensor(small[:, 2, 0:k], small[:, 4, 0:k], small[:, 1, 0:k], ALU.add).then_inc(s_var, 1)

            def unit_a(u, j, p):
                dve.wait_ge(b_x[p], 16 * (j + 1))
                dve.scalar_tensor_tensor(xb[:, p, :], xb[:, p, :], 0.0, xb[:, p, :], ALU.max, ALU.add).then_inc(b_z, 1)
                dve.wait_ge(b_z, u + 1)
                moments(xb[:, p, :], G, b_bn, b_q, b_var, u)

            def unit_b(u, j, p):
                dve.wait_ge(b_std, u + 1)
                dve.reciprocal(small[:, 7, :], small[:, 3, :]).then_inc(b_r, 1)
                ge(dve, b_T, 2 * u)
                dve.wait_ge(b_r, u + 1)
                dve.tensor_tensor(tiles(yb[:, :], G), tiles(xb[:, p, :], G), spread(small[:, 7, :], G), ALU.mult).then_inc(b_y, 1)

            def unit_sums(u, j, p):
                dve.wait_ge(b_sq, 2 * u + 2)
                dve.tensor_reduce(small[:, 5, :], tiles(sq[:, :], G), AX.X, ALU.add).then_inc(b_red, 1)

            def unit_out(u, j, p, PC):
                dve.wait_ge(b_std2, u + 1)
                ge(dve, b_out, u)
                dve.reciprocal(small[:, 0, :], small[:, 6, :]).then_inc(b_r2, 1)
                ge(dve, b_st[p], 16 * j)
                dve.wait_ge(b_r2, u + 1)
                dve.tensor_tensor(tiles(ob[:, p, :], G), tiles(PC[:, :], G), spread(small[:, 0, :], G), ALU.mult).then_inc(b_out, 1)

            def difference(i, j, p):
                dve.wait_ge(e_g[p], 128 * (j + 1))
                ge(dve, e_T, i)
                dve.tensor_tensor(dx[:, :], g1[:, p, CH:2 * CH], g1[:, p, 0:CH], ALU.subtract).then_inc(e_dd, 1)

            def edge_stats(i, j, p):
                dve.wait_ge(e_c, i + 1)
                end = isinstance(i, int) and i == CHUNKS - 1
                dve.bn_stats(bnE[:, i, :] if isinstance(i, int) else bnE[:, bass.ds(i, 1), :].rearrange("p a n -> p (a n)"),
                             edge_cols[:, bass.ds(i * CH, LASTN if end else CH)]).then_inc(e_bn, 1)

            def edge1(i, j, p):
                first = isinstance(i, int) and i == 0
                if not first:
                    difference(*prev(i, j, p))
                if not (isinstance(i, int) and i < 2):
                    unit_sums(i - 2, j - 1, p)
                    unit_out(i - 2, j - 1, p, PC)
                unit_a(i, j, p)
                if not first:
                    edge_stats(*prev(i, j, p))
                unit_b(i, j, p)
            steps(dve, 0, CHUNKS, edge1)
            difference(*final)
            unit_sums(*prev(*final))
            unit_out(*prev(*final), PC)
            edge_stats(*final)

            def norm(g, b, k):
                dve.wait_ge(e_bn, (k + 1) * CHUNKS)
                dve.bn_aggr(mvE[:, 0:2], bnE[:, :, :].rearrange("p n s -> p (n s)")).then_inc(m_aff, 1)
                dve.wait_ge(m_st, k + 1)
                link(dve.reciprocal(mvE[:, 5:6], mvE[:, 2:3]))
                dve.tensor_tensor(mvE[:, 3:4], mvE[:, 5:6], par[:, g:g + 1], ALU.mult).then_inc(m_aff, 1)
                dve.wait_ge(m_aff, 3 * k + 2)
                link(dve.tensor_tensor(mvE[:, 6:7], mvE[:, 0:1], mvE[:, 3:4], ALU.mult))
                dve.tensor_tensor(mvE[:, 4:5], par[:, b:b + 1], mvE[:, 6:7], ALU.subtract).then_inc(m_aff, 1)

            norm(0, 1, 0)

            def edge2(i, j, p):
                dve.wait_ge(f_mm, i + 1)
                end = isinstance(i, int) and i == CHUNKS - 1
                dve.bn_stats(bnE[:, i, :] if isinstance(i, int) else bnE[:, bass.ds(i, 1), :].rearrange("p a n -> p (a n)"),
                             PE_[p][:, 0:LASTN if end else CH]).then_inc(e_bn, 1)
                dve.tensor_copy(edge_cols[:, cols(i)], PE_[p][:, :]).then_inc(f_c, 1)
            steps(dve, 0, CHUNKS, edge2, tail=1)
            dve.wait_ge(f_c, CHUNKS)
            norm(2, 3, 1)

            def mean0(i, j, p):
                dve.wait_ge(k_T, i + 1)
                ge(dve, k_st[p], 16 * j)
                dve.tensor_tensor(tiles(tr[:, p, :], T), tiles(PE_[p][:, :], T),
                                  spread(inv_cnt[:, bass.ds(i * T, T)], T), ALU.mult).then_inc(k_m, 1)

            dve.wait_ge(s_sameb, 32)

            def edge3(i, j, p):
                dve.wait_ge(k_r, i + 1)
                ge(dve, k_T, i - 1)
                ge(dve, k_sc, i)
                first = isinstance(i, int) and i == 0
                dve.tensor_tensor_scan(sc[:, p, :], same[:, cols(i)], rl[:, p, :],
                                       0.0 if first else sc[:, 1 - p, CH - 1:CH], ALU.mult, ALU.add).then_inc(k_sc, 1)
                if not first:
                    mean0(*prev(i, j, p))
            steps(dve, 0, CHUNKS, edge3)
            mean0(*final)

            def dense(u, j, p):
                if isinstance(u, int) and u == CHUNKS + 1:
                    unit_sums(*final)
                unit_a(u, j, p)
                if not (isinstance(u, int) and u == CHUNKS):
                    unit_out(u - 2, j - 1, p, (PC, PD)[p])
                unit_b(u, j, p)
            steps(dve, CHUNKS, UNITS, dense)
            unit_out(*prev(*final_unit), PC)
            unit_out(*final_unit, PD)

            def sum1(i, j, p):
                dve.wait_ge(l_ev, 2 * i + 1)
                ge(dve, l_t, i - 1)
                ge(dve, l_sc, i)
                first = isinstance(i, int) and i == 0
                dve.tensor_tensor_scan(sc[:, p, :], same[:, cols(i)], edge_cols[:, cols(i)],
                                       0.0 if first else sc[:, 1 - p, CH - 1:CH], ALU.mult, ALU.add).then_inc(l_sc, 1)

            def t1(i, j, p):
                dve.wait_ge(l_t, i + 1)
                ge(dve, l_tst[p], 16 * j)
                ge(dve, l_h, i - 1)
                dve.tensor_tensor(tiles(tr[:, p, :], T), tiles(PE_[0][:, :], T),
                                  spread(inv_cnt[:, bass.ds(i * T, T)], T), ALU.mult).then_inc(l_tu, 1)

            def edge5(i, j, p):
                first = isinstance(i, int) and i == 0
                dve.wait_ge(l_ld[p], 48 * (j + 1))
                dve.wait_ge(l_g[p], 64 * (j + 1))
                ge(dve, l_y, i)
                ge(dve, l_y2, i)
                dve.tensor_tensor(hT[:, :], xb[:, p, :], ob[:, p, :], ALU.add).then_inc(l_z, 1)
                dve.wait_ge(l_z, i + 1)
                dve.scalar_tensor_tensor(sq[:, :], hT[:, :], 0.0, xb[:, p, :], ALU.max, ALU.add).then_inc(l_x, 1)
                dve.wait_ge(l_x, i + 1)
                moments(sq[:, :], G, l_bn, l_q, l_var, i, None if first else lambda: sum1(*prev(i, j, p)))
                dve.wait_ge(l_std, i + 1)
                dve.reciprocal(small[:, 7, :], small[:, 3, :]).then_inc(l_r, 1)
                ge(dve, l_T, 2 * i - 1)
                dve.wait_ge(l_r, i + 1)
                dve.tensor_tensor(tiles(half(yb, 0), T), tiles(half(sq, 0), T), spread(small[:, 7, 0:T], T), ALU.mult).then_inc(l_y, 1)
                if not first:
                    t1(*prev(i, j, p))
            steps(dve, 0, CHUNKS, edge5)
            sum1(*final)
            t1(*final)
            dve.wait_ge(l_bst[0], 16 * ((CHUNKS + 1) // 2))
            dve.wait_ge(l_bst[1], 16 * (CHUNKS // 2))
            dve.wait_ge(l_tst[0], 16 * ((CHUNKS + 1) // 2))
            dve.wait_ge(l_tst[1], 16 * (CHUNKS // 2))

            def sum_squares(i, j, p):
                dve.wait_ge(o_sq, i + 1)
                dve.tensor_reduce(small[:, 5, 0:T], tiles(half(sq, p), T), AX.X, ALU.add).then_inc(o_red, 1)

            def normalise(i, j, p):
                dve.wait_ge(o_std, i + 1)
                dve.reciprocal(small[:, 7, 0:T], small[:, 6, 0:T]).then_inc(o_rs, 1)
                ge(dve, o_st[p], 64 * j)
                dve.wait_ge(o_rs, i + 1)
                dve.tensor_tensor(tiles(ob[:, p, 0:CH], T), tiles(tr[:, p, :], T), spread(small[:, 7, 0:T], T), ALU.mult).then_inc(o_out, 1)

            def edge6(i, j, p):
                first = isinstance(i, int) and i == 0
                if not first:
                    sum_squares(*prev(i, j, p))
                    normalise(*prev(i, j, p))
                dve.wait_ge(o_r, i + 1)
                ge(dve, o_a, i - 1)
                ge(dve, o_sc, i)
                dve.tensor_tensor_scan(sc[:, p, :], same[:, cols(i)], rl[:, p, :],
                                       0.0 if first else sc[:, 1 - p, CH - 1:CH], ALU.mult, ALU.add).then_inc(o_sc, 1)
                dve.wait_ge(o_a, i + 1)
                dve.tensor_tensor(tiles(dx[:, :], T), tiles(PE_[1][:, :], T),
                                  spread(inv_cnt[:, bass.ds(i * T, T)], T), ALU.mult).then_inc(o_m, 1)
                dve.wait_ge(o_b[p], 16 * (j + 1))
                dve.wait_ge(o_m, i + 1)
                dve.tensor_tensor(tr[:, p, :], dx[:, :], xb[:, p, 0:CH], ALU.add).then_inc(o_z, 1)
            steps(dve, 0, CHUNKS, edge6)
            sum_squares(*final)
            normalise(*final)


_NAMES = ['x', 'src', 'dst', 'L0_gnn_theta_w', 'L0_gnn_phi_w', 'L0_gnn_fc1_w', 'L0_gnn_bn0_g', 'L0_gnn_bn0_b',
          'L0_gnn_bn1_g', 'L0_gnn_bn1_b', 'L1_gnn_W1l', 'L1_gnn_b1l', 'L1_gnn_W1r', 'L1_gnn_W2l', 'L1_gnn_b2l',
          'L1_gnn_W2r']


def kernel(**inputs):
    import numpy as _np
    import concourse.bacc as _bacc
    from concourse import mybir as _mybir
    from concourse.bass_utils import run_bass_kernel_spmd as _run

    nc = _bacc.Bacc("TRN2", target_bir_lowering=False, num_devices=1)
    arrays, args = {}, []
    for name in _NAMES:
        a = _np.ascontiguousarray(inputs[name])
        arrays[f"in_{name}"] = a
        args.append(nc.dram_tensor(f"in_{name}", a.shape, _mybir.dt.from_np(a.dtype), kind="ExternalInput").ap())
    shape = inputs['x'].shape
    args.append(nc.dram_tensor("out_rows", shape, _mybir.dt.float32, kind="ExternalOutput").ap())
    gnn_program(nc, *args)
    r = _run(nc, [arrays], core_ids=[0])
    return r.results[0]["out_rows"]
```
